# Optimizing a Trainium2 kernel written in Bass

```python
import numpy as np
import jax
import jax.numpy as jnp

def _softmax(x, axis=-1):
    return jax.nn.softmax(x, axis=axis)

def _gelu(x):
    return jax.nn.gelu(x, approximate=True)

def _silu(x):
    return jax.nn.silu(x)

def _sigmoid(x):
    return jax.nn.sigmoid(x)

def _layernorm(x, axis=-1, eps=1e-05):
    m = jnp.mean(x, axis=axis, keepdims=True)
    v = jnp.var(x, axis=axis, keepdims=True)
    return (x - m) / jnp.sqrt(v + eps)

def _scatter_add(tgt, idx, src, axis=0):
    return tgt.at[idx].add(src)

def _segment_sum(src, seg, n):
    return jax.ops.segment_sum(src, seg, n)
kernel_name = 'mk_adaln_d1_jaxref_r8_da5f3d'

def setup_inputs(seed: int=0):
    np.random.seed(seed)
    _w = jnp.asarray

    def _L0_attn_setup():
        import jax, jax.numpy as jnp
        import numpy as np
        D_MODEL, H, DK, DV = (128, 16, 64, 64)
        key = jax.random.key(seed)
        ks = jax.random.split(key, 9)
        s = lambda fan_in: 1.0 / np.sqrt(fan_in)
        return {'x': jax.random.normal(ks[0], (2, 256, D_MODEL), dtype=jnp.float32), 'Wq': jax.random.uniform(ks[1], (D_MODEL, H * DK), jnp.float32, -s(D_MODEL), s(D_MODEL)), 'bq': jax.random.uniform(ks[2], (H * DK,), jnp.float32, -s(D_MODEL), s(D_MODEL)), 'Wk': jax.random.uniform(ks[3], (D_MODEL, DK), jnp.float32, -s(D_MODEL), s(D_MODEL)), 'bk': jax.random.uniform(ks[4], (DK,), jnp.float32, -s(D_MODEL), s(D_MODEL)), 'Wv': jax.random.uniform(ks[5], (D_MODEL, DV), jnp.float32, -s(D_MODEL), s(D_MODEL)), 'bv': jax.random.uniform(ks[6], (DV,), jnp.float32, -s(D_MODEL), s(D_MODEL)), 'Wo': jax.random.uniform(ks[7], (H * DV, D_MODEL), jnp.float32, -s(H * DV), s(H * DV)), 'bo': jax.random.uniform(ks[8], (D_MODEL,), jnp.float32, -s(H * DV), s(H * DV))}
    _L0_attn_in = _L0_attn_setup()

    def _L0_ffn_setup():
        import jax, jax.numpy as jnp
        import numpy as np
        HID = 128
        NH = 16
        NKV = 4
        HD = HID // NH
        E = 8
        TOPK = 2
        FFN = 256
        EPS = 1e-05
        THETA = 10000.0

        def _rmsnorm(x, w):
            var = jnp.mean(x * x, axis=-1, keepdims=True)
            return x * jax.lax.rsqrt(var + EPS) * w

        def _rope_tables(S):
            inv_freq = 1.0 / THETA ** (jnp.arange(0, HD, 2, dtype=jnp.float32) / HD)
            freqs = jnp.arange(S, dtype=jnp.float32)[:, None] * inv_freq[None, :]
            emb = jnp.concatenate([freqs, freqs], axis=-1)
            return (jnp.cos(emb), jnp.sin(emb))

        def _apply_rope(t, cos, sin):
            t1, t2 = jnp.split(t, 2, axis=-1)
            rot = jnp.concatenate([-t2, t1], axis=-1)
            return t * cos[None, :, None, :] + rot * sin[None, :, None, :]
        key = jax.random.key(seed)
        ks = jax.random.split(key, 6)
        B, S = (1, 256)
        x = jax.random.normal(ks[0], (B, S, HID), dtype=jnp.float32)
        wqkv = jax.random.normal(ks[1], ((NH + 2 * NKV) * HD, HID), dtype=jnp.float32) * 0.02
        wo = jax.random.normal(ks[2], (HID, NH * HD), dtype=jnp.float32) * 0.02
        gate_w = jax.random.normal(ks[3], (E, HID), dtype=jnp.float32) * 0.02
        w13 = jax.random.normal(ks[4], (E, 2 * FFN, HID), dtype=jnp.float32) * 0.02
        w2 = jax.random.normal(ks[5], (E, HID, FFN), dtype=jnp.float32) * 0.02
        return {'x': x, 'ln1_w': jnp.ones((HID,), jnp.float32), 'ln2_w': jnp.ones((HID,), jnp.float32), 'wqkv': wqkv, 'wo': wo, 'gate_w': gate_w, 'w13': w13, 'w2': w2}
    _L0_ffn_in = _L0_ffn_setup()
    _L0_c = _w((lambda *s: np.random.randn(*s).astype(np.float32) * 0.05)(2, 128))
    _L0_wmod = _w((lambda *s: np.random.randn(*s).astype(np.float32) * 0.05)(128, 6 * 128) * 128 ** (-0.5))
    _d = {'L0_attn_x': _L0_attn_in['x'], 'L0_attn_Wq': _L0_attn_in['Wq'], 'L0_attn_bq': _L0_attn_in['bq'], 'L0_attn_Wk': _L0_attn_in['Wk'], 'L0_attn_bk': _L0_attn_in['bk'], 'L0_attn_Wv': _L0_attn_in['Wv'], 'L0_attn_bv': _L0_attn_in['bv'], 'L0_attn_Wo': _L0_attn_in['Wo'], 'L0_attn_bo': _L0_attn_in['bo'], 'L0_ffn_ln1_w': _L0_ffn_in['ln1_w'], 'L0_ffn_ln2_w': _L0_ffn_in['ln2_w'], 'L0_ffn_wqkv': _L0_ffn_in['wqkv'], 'L0_ffn_wo': _L0_ffn_in['wo'], 'L0_ffn_gate_w': _L0_ffn_in['gate_w'], 'L0_ffn_w13': _L0_ffn_in['w13'], 'L0_ffn_w2': _L0_ffn_in['w2'], 'L0_c': _L0_c, 'L0_wmod': _L0_wmod}
    _x0 = _d['L0_attn_x']
    _d['L0_attn_x'] = jax.random.normal(jax.random.fold_in(jax.random.key(seed), 1), (2, 1024, 128), dtype=_x0.dtype)
    del _x0
    return _d

def reference(L0_attn_x, L0_attn_Wq, L0_attn_bq, L0_attn_Wk, L0_attn_bk, L0_attn_Wv, L0_attn_bv, L0_attn_Wo, L0_attn_bo, L0_ffn_ln1_w, L0_ffn_ln2_w, L0_ffn_wqkv, L0_ffn_wo, L0_ffn_gate_w, L0_ffn_w13, L0_ffn_w2, L0_c, L0_wmod):

    def _L0_attn_ref(x, Wq, bq, Wk, bk, Wv, bv, Wo, bo):
        import jax, jax.numpy as jnp
        import numpy as np
        D_MODEL, H, DK, DV = (128, 16, 64, 64)
        B, S, _ = x.shape
        q = (x @ Wq + bq).reshape(B, S, H, DK)
        k = x @ Wk + bk
        v = x @ Wv + bv
        scores = jnp.einsum('bshd,btd->bhst', q, k) / np.sqrt(DK).astype(x.dtype)
        w = jax.nn.softmax(scores, axis=-1)
        out = jnp.einsum('bhst,btd->bshd', w, v).reshape(B, S, H * DV)
        return out @ Wo + bo

    def _L0_ffn_ref(x, ln1_w, ln2_w, wqkv, wo, gate_w, w13, w2):
        import jax, jax.numpy as jnp
        import numpy as np
        HID = 128
        NH = 16
        NKV = 4
        HD = HID // NH
        E = 8
        TOPK = 2
        FFN = 256
        EPS = 1e-05
        THETA = 10000.0

        def _rmsnorm(x, w):
            var = jnp.mean(x * x, axis=-1, keepdims=True)
            return x * jax.lax.rsqrt(var + EPS) * w

        def _rope_tables(S):
            inv_freq = 1.0 / THETA ** (jnp.arange(0, HD, 2, dtype=jnp.float32) / HD)
            freqs = jnp.arange(S, dtype=jnp.float32)[:, None] * inv_freq[None, :]
            emb = jnp.concatenate([freqs, freqs], axis=-1)
            return (jnp.cos(emb), jnp.sin(emb))

        def _apply_rope(t, cos, sin):
            t1, t2 = jnp.split(t, 2, axis=-1)
            rot = jnp.concatenate([-t2, t1], axis=-1)
            return t * cos[None, :, None, :] + rot * sin[None, :, None, :]
        B, S, _ = x.shape
        h = _rmsnorm(x, ln1_w)
        qkv = jnp.einsum('bsh,oh->bso', h, wqkv)
        q = qkv[..., :NH * HD].reshape(B, S, NH, HD)
        k = qkv[..., NH * HD:(NH + NKV) * HD].reshape(B, S, NKV, HD)
        v = qkv[..., (NH + NKV) * HD:].reshape(B, S, NKV, HD)
        cos, sin = _rope_tables(S)
        q = _apply_rope(q, cos, sin)
        k = _apply_rope(k, cos, sin)
        groups = NH // NKV
        k = jnp.repeat(k, groups, axis=2)
        v = jnp.repeat(v, groups, axis=2)
        scale = HD ** (-0.5)
        scores = jnp.einsum('bqhd,bkhd->bhqk', q, k) * scale
        causal = jnp.tril(jnp.ones((S, S), dtype=bool))
        scores = jnp.where(causal[None, None], scores, jnp.finfo(scores.dtype).min)
        probs = jax.nn.softmax(scores, axis=-1)
        attn = jnp.einsum('bhqk,bkhd->bqhd', probs, v).reshape(B, S, NH * HD)
        x = x + jnp.einsum('bso,ho->bsh', attn, wo)
        h = _rmsnorm(x, ln2_w).reshape(-1, HID)
        T = h.shape[0]
        logits = jnp.einsum('th,eh->te', h, gate_w)
        rprobs = jax.nn.softmax(logits.astype(jnp.float32), axis=-1)
        topw, topi = jax.lax.top_k(rprobs, TOPK)
        topw = topw / jnp.sum(topw, axis=-1, keepdims=True)
        wfull = jnp.zeros((T, E), jnp.float32).at[jnp.arange(T)[:, None], topi].set(topw)
        wfull = wfull.astype(h.dtype)
        out = jnp.zeros((T, HID), h.dtype)
        for e in range(E):
            w1 = w13[e, :FFN]
            w3 = w13[e, FFN:]
            g = jax.nn.silu(h @ w1.T) * (h @ w3.T)
            out = out + jnp.einsum('tf,hf->th', g, w2[e]) * wfull[:, e:e + 1]
        return x + out.reshape(B, S, HID)
    x = L0_attn_x
    mod = (_silu(L0_c) @ L0_wmod).reshape(L0_c.shape[0], 6, 1, -1)
    sa, ca, ga, sb, cb, gb = (mod[:, 0], mod[:, 1], mod[:, 2], mod[:, 3], mod[:, 4], mod[:, 5])
    ga = (2 * (ga >= 0) - 1) * jnp.maximum(jnp.abs(ga), 0.25)
    gb = (2 * (gb >= 0) - 1) * jnp.maximum(jnp.abs(gb), 0.25)
    h = _layernorm(x, axis=-1) * (1 + ca) + sa
    x = x + ga * _L0_attn_ref(h, L0_attn_Wq, L0_attn_bq, L0_attn_Wk, L0_attn_bk, L0_attn_Wv, L0_attn_bv, L0_attn_Wo, L0_attn_bo)
    h = _layernorm(x, axis=-1) * (1 + cb) + sb
    x = x + gb * _L0_ffn_ref(h, L0_ffn_ln1_w, L0_ffn_ln2_w, L0_ffn_wqkv, L0_ffn_wo, L0_ffn_gate_w, L0_ffn_w13, L0_ffn_w2)
    return x

_drawn_inputs = setup_inputs


def setup_inputs(seed=0):
    import zlib

    import numpy as np

    out = dict(_drawn_inputs(seed))
    spreads = {'L0_ffn_ln1_w': (1.0, 0.6), 'L0_ffn_ln2_w': (1.0, 0.6)}
    factors = {'L0_attn_Wq': 8.0,
     'L0_attn_bq': 8.0,
     'L0_attn_Wk': 8.0,
     'L0_attn_bk': 8.0,
     'L0_attn_Wv': 8.0,
     'L0_attn_bv': 6.476,
     'L0_attn_Wo': 5.558,
     'L0_attn_bo': 8.0,
     'L0_ffn_wqkv': 8.0,
     'L0_ffn_wo': 8.0,
     'L0_ffn_gate_w': 8.0,
     'L0_ffn_w13': 8.0,
     'L0_ffn_w2': 8.0}
    for name, (base, spread) in spreads.items():
        noise = np.random.default_rng([zlib.crc32(name.encode()), seed]).standard_normal(out[name].shape)
        drawn = base * np.exp(spread * noise) if base else spread * noise
        out[name] = jnp.asarray(drawn.astype(out[name].dtype))
    for name, factor in factors.items():
        out[name] = (out[name] * factor).astype(out[name].dtype)
    return out
```

```python
from contextlib import ExitStack

import concourse.bass as bass
from concourse import mybir

F32 = mybir.dt.float32
F32R = mybir.dt.float32r
ALU = mybir.AluOpType
ACT = mybir.ActivationFunctionType
AX_X = mybir.AxisListType.X

B, S, D = 2, 1024, 128
NT = S // 128
NC = 2
CH = S // NC
H, DK = 16, 64
PAIRS = H // 2
UNITS = 4
STEPS = 4
NG, HPG, HD = 4, 4, 8
NH2 = NG * HPG
QKV = (NH2 + 2 * NG) * HD
ROWS = 32
MROW = 24
ITEMS = 48
ST2 = 24
PV2 = 12
E, FFN = 8, 256
EPS = 1e-5
LOW = -1.0e30
DVE_STEPS = 175
DVE_PAIR = 12
DVE_J = 5


class Chain:

    def __init__(self, eng, sem):
        self.eng, self.sem, self.n, self.base = eng, sem, 0, 0

    def link(self, ins):
        self.n += 1
        ins.then_inc(self.sem, 1)
        self.eng.wait_ge(self.sem, self.base + self.n)


def rows(n):
    c, kt = n
    off = max(0, kt * 128 - c * CH)
    return off, CH - off


def item(t, g, piece):
    return 4 * t + g if t < 4 else 16 + 8 * (t - 4) + 2 * g + piece


def pieces():
    for t in range(NT):
        for g in range(NG):
            if t >= 4:
                yield t, g, 0, 0, CH
            yield t, g, 1, CH * (t // 4), (t % 4 + 1) * 128


def build(nc, a_x, Wq, bq, Wk, bk, Wv, bv, Wo, bo, ln1, ln2, wqkv, wo, gate, w13, w2, cin, wmod, rope, out):
    with ExitStack() as ctx:
        def sb(name, shape, dt=F32):
            return ctx.enter_context(nc.sbuf_tensor(name, shape, dt))

        def ps(name, shape):
            return ctx.enter_context(nc.psum_tensor(name, shape, F32))

        def sem(name):
            return ctx.enter_context(nc.semaphore(name))

        SC = ps("SC", [128, 2, 1024])
        SCF = SC[:, :, :].rearrange("p a b -> p (a b)")
        MX = ps("MX", [128, 1024])
        PV = ps("PV", [128, CH])
        XP = ps("XP", [128, CH])

        ident = sb("ident", [128, 128])
        tri = sb("tri", [128, CH])
        wk2 = sb("wk2", [128, 128])
        wvs = sb("wvs", [128, DK])
        wos = sb("wos", [128, PAIRS, D])
        bqs = sb("bqs", [128, PAIRS])
        bks = sb("bks", [128, 1])
        bvs = sb("bvs", [128, DK])
        bos = sb("bos", [128, 1])
        lns = sb("lns", [128, 2, D])
        cs = sb("cs", [128, B])
        csil = sb("csil", [128, B])
        cbc = sb("cbc", [128, B, 128])
        wmods = sb("wmods", [128, 6 * D])
        mods = sb("mods", [128, B, 6, D])
        gsgn = sb("gsgn", [128, D])
        gates = sb("gates", [128, E])
        ropes = sb("ropes", [128, NT, 2, HD])
        BIG = sb("BIG", [128, PAIRS * S])
        AT = BIG[:, :].rearrange("p (j n) -> p j n", j=PAIRS)
        W13T = sb("W13T", [128, E, 2 * FFN])
        W2T = sb("W2T", [128, E, 2 * D])
        WQKVT = sb("WQKVT", [128, QKV])
        WOT = sb("WOT", [128, D])

        X = sb("X", [128, NT, D])
        X1 = sb("X1", [128, NT, D])
        HA = sb("HA", [128, NT, D])
        H2 = sb("H2", [128, NT, D])
        TA = sb("TA", [128, NT, D])
        TB = sb("TB", [128, NT, D])
        HT = sb("HT", [128, S])
        st = sb("st", [128, 8, NT])
        wqs = sb("wqs", [128, 128])
        KK = sb("KK", [128, S], F32R)
        KL = sb("KL", [128, S], F32R)
        V1 = sb("V1", [128, NT, 128])
        QF = sb("QF", [128, CH])
        QS = [sb(f"QS{i}", [128, CH], F32R) for i in range(2)]
        Q2 = [sb(f"Q2{i}", [128, CH], F32R) for i in range(2)]
        MC = sb("MC", [128, STEPS])
        MR = sb("MR", [STEPS, 128], F32R)
        P = sb("P", [128, 2, NG, CH])
        LD = sb("LD", [64, CH])
        RD = sb("RD", [64, CH])
        N1 = sb("N1", [64, CH])
        qkv = sb("qkv", [128, NT, QKV])
        qkr = sb("qkr", [128, NT, QKV - NG * HD])
        qko = sb("qko", [128, NT, QKV - NG * HD])
        QSJ = sb("QSJ", [128, NT, NG, ROWS], F32R)
        KT = sb("KT", [128, NG, S], F32R)
        QTA = sb("QTA", [128, S], F32R)
        QTB = sb("QTB", [128, S], F32R)
        V2 = sb("V2", [128, NT, NG, ROWS])
        M2 = sb("M2", [128, NT, NG, 2])
        RC = sb("RC", [128, 4, NG])
        L8 = sb("L8", [128, NT, E])
        T8 = sb("T8", [128, NT, 8])
        I8 = sb("I8", [128, NT, 8], mybir.dt.uint32)
        IF = sb("IF", [128, NT, 2])
        io8 = sb("io8", [128, E])
        WF = sb("WF", [128, NT, E])
        W8 = sb("W8", [128, NT, E])
        W13S = [sb(f"W13S{i}", [128, 2 * FFN]) for i in range(2)]
        W2S = [sb(f"W2S{i}", [128, 2 * D]) for i in range(2)]
        AO = TB
        KS = QSJ
        SG = P[:, 0, 0:2, :]
        G = P[:, 1, :, :].rearrange("p (c f) q -> p c f q", c=NC)
        ACC = BIG[:, 0:S].rearrange("p (t d) -> p t d", t=NT)
        OV = BIG[:, S:S + CH]
        junk = BIG[:, 2 * S:6 * S].rearrange("p (n q) -> p n q", n=8)

        names = """small rawld wmodld idn tri io const one turn csil cbc mod mods xld wqld dve var r0
            h hT hTc kv kvx q qf qs mx mred mt mrow mdma main exp pv rd norm a1 op opc opT x1 h3 h3T h3Tc qkv
            qkvc ks kT kTc vset qsj ta qta m2 m2red qsm tb qtb main2 exp2 tri2 pv2 ovc ov ovt ao aoT aoTc wo2 h4 h4T
            h4Tc lg rt slot wcopy up silu g down accfree y out""".split()
        s = {n: sem("s_" + n) for n in names}
        block = ctx.enter_context(nc.Block())

        def bc(ap, n=NT):
            return ap.unsqueeze(1).to_broadcast([128, n, ap.shape[-1]])

        def per_token(ap, n=D):
            return ap.unsqueeze(2).to_broadcast([128, ap.shape[1], n])

        def tiles(ap):
            return ap.rearrange("p (t d) -> p t d", d=128)

        def plain(eng):
            eng.sem_inc(s["turn"], 1)

        STARTED = {n: 1 for n in "x1 q h4T op mt mrow mred qs norm tb m2red ovt ov ao mods main".split()} | {"mdma": 16, "out": 16}

        @block.sync
        def _(sp):
            for n, turn in STARTED.items():
                sp.sem_inc(s[n], turn)
            sp.dma_start(cs[:, :], cin).then_inc(s["wmodld"], 16)
            sp.dma_start(wmods[:, :], wmod).then_inc(s["wmodld"], 16)
            small = [
                (wk2[:, 0:DK], Wk), (wk2[:, DK:128], Wk), (wvs[:, :], Wv),
                (wos[:, :, :], Wo.rearrange("(j p) d -> p j d", p=128)),
                (bqs[:, :], bq),
                (bks[0:64, :], bk.rearrange("(p a) -> p a", a=1)), (bks[64:128, :], bk.rearrange("(p a) -> p a", a=1)),
                (bvs[:, :], bv.partition_broadcast(128)), (bos[:, :], bo.rearrange("(p a) -> p a", a=1)),
                (lns[:, 0, :], ln1.partition_broadcast(128)), (lns[:, 1, :], ln2.partition_broadcast(128)),
                (gates[:, :], gate), (WQKVT[:, :], wqkv), (WOT[:, :], wo),
                (ropes[:, :, :, :], rope.rearrange("(t p) k d -> p t k d", p=128)),
            ]
            for dst, src in small:
                sp.dma_start(dst, src).then_inc(s["small"], 16)
            sp.dma_start(W13T[:, :, :], w13).then_inc(s["rawld"], 16)
            sp.dma_start(W2T[:, :, :], w2).then_inc(s["rawld"], 16)
            with sp.Fori(0, B) as b:
                sp.wait_ge(s["x1"], 1 + b)
                sp.dma_start(X[:, :, :], a_x[b].rearrange("(t p) d -> p t d", p=128)).then_inc(s["xld"], 16)
                sp.wait_ge(s["q"], 1 + b * (2 * PAIRS))
                sp.dma_start(wqs[:, :], Wq[:, 0:128]).then_inc(s["wqld"], 16)

                def max_row(unit, q2):
                    sp.wait_ge(s["mrow"], 1 + unit + 1)
                    sp.dma_start(q2[64:65, :].bitcast(F32), MR[:, :].bitcast(F32)).then_inc(s["mdma"], 16)

                def pair_rows(p, last):
                    unit = b * (PAIRS * UNITS) + p * UNITS
                    max_row(unit + 1, Q2[1])
                    max_row(unit + 2, Q2[0])
                    max_row(unit + 3, Q2[1])
                    if not last:
                        sp.wait_ge(s["q"], 1 + b * (2 * PAIRS) + p * 2 + 2)
                        sp.dma_start(wqs[:, :], Wq[:, bass.ds(p * 128 + 128, 128)]).then_inc(s["wqld"], 16)
                        max_row(unit + 4, Q2[0])

                max_row(b * (PAIRS * UNITS), Q2[0])
                with sp.Fori(0, PAIRS - 1) as p:
                    pair_rows(p, False)
                pair_rows(PAIRS - 1, True)
                sp.wait_ge(s["y"], b + 1)
                sp.dma_start(out[b].rearrange("(t p) d -> p t d", p=128), TA[:, :, :]).then_inc(s["out"], 16)
            sp.wait_ge(s["out"], 16 + 16 * B)

        @block.gpsimd
        def _(pool):
            pool.memset(ident[:, :], 0.0).then_inc(s["idn"], 1)
            pool.memset(tri[:, :], 0.0).then_inc(s["idn"], 1)
            pool.wait_ge(s["idn"], 2)
            pool.affine_select(out=ident[:, :], in_=ident[:, :], compare_op=ALU.not_equal, fill=1.0, base=0,
                               pattern=[[-1, 128]], channel_multiplier=1).then_inc(s["idn"], 1)
            pool.affine_select(out=tri[:, CH - 128:CH], in_=tri[:, CH - 128:CH], compare_op=ALU.is_ge, fill=LOW,
                               base=0, pattern=[[-1, 128]], channel_multiplier=1).then_inc(s["tri"], 1)
            pool.iota(io8[:, :], pattern=[[1, E]], base=0, channel_multiplier=0,
                      allow_small_or_imprecise_dtypes=True).then_inc(s["io"], 1)
            pool.memset(W13S[0][:, 0:1], 0.0).then_inc(s["slot"], 2)
            pool.memset(W13S[1][:, 0:1], 0.0).then_inc(s["accfree"], 2)
            pool.wait_ge(s["slot"], 2)
            pool.wait_ge(s["accfree"], 2)
            pool.wait_ge(s["rawld"], 32)
            with pool.Fori(0, B) as b:
                with pool.Fori(0, HPG) as j:
                    n = 0
                    for c in range(NC):
                        for kt in range(4 * c, 4 * c + 4):
                            stp = (8 if c else 0) + 2 * kt
                            off, _ = rows((c, kt))
                            for hh in range(2):
                                pool.wait_ge(s["exp2"], (b * HPG + j) * ST2 + stp + hh + 1)
                                plain(pool)
                                blk = P[:, (4 * c + kt) % 2, 2 * hh:2 * hh + 2, off:off + 128]
                                pool.affine_select(out=blk, in_=blk, compare_op=ALU.is_ge, fill=0.0, base=0,
                                                   pattern=[[0, 2], [1, 128]], channel_multiplier=-1).then_inc(s["tri2"], 1)
                                n += 1
                with pool.Fori(0, E // 2) as ee:
                    for k in range(2):
                        pool.wait_ge(s["slot"], b * E + ee * 2 + k + 1)
                        plain(pool)
                        pool.tensor_copy(W13S[k][:, :], W13T[:, ee * 2 + k, :])
                        pool.tensor_copy(W2S[k][:, :], W2T[:, ee * 2 + k, :]).then_inc(s["wcopy"], 1)

        @block.scalar
        def _(act):
            act.wait_ge(s["wmodld"], 32)
            act.activation(csil[:, :], cs[:, :], ACT.Silu).then_inc(s["csil"], 1)
            act.wait_ge(s["small"], 16 * 15)
            with act.Fori(0, B) as b:
                def inverse_root(k):
                    act.wait_ge(s["var"], b * 4 + k + 1)
                    act.activation(st[:, 3, :], st[:, 2, :], ACT.Ln).then_inc(s["r0"], 1)
                    act.wait_ge(s["r0"], b * 8 + 2 * k + 1)
                    act.activation(st[:, 4, :], st[:, 3, :], ACT.Exp, scale=-0.5).then_inc(s["r0"], 1)

                def exps(unit, t):
                    act.wait_ge(s["main"], 1 + unit * STEPS + t + 1)
                    if t >= 2:
                        act.wait_ge(s["pv"], unit * STEPS + t - 1)
                    act.activation(P[:, t % 2, 0:2, :].rearrange("p a b -> p (a b)"), SC[:, t % 2, :], ACT.Exp,
                                   scale=DK ** -0.5).then_inc(s["exp"], 1)

                def q_out(p, c):
                    act.wait_ge(s["q"], 1 + b * (2 * PAIRS) + p * 2 + c + 1)
                    act.wait_ge(s["qs"], 1 + (b * (2 * PAIRS) + p * 2 + c) * 2)
                    act.activation(QF[:, :], XP[:, :], ACT.Identity, bias=bqs[:, bass.ds(p, 1)]).then_inc(s["qf"], 1)

                def unit_acts(p, u, last):
                    unit = b * (PAIRS * UNITS) + p * UNITS + u
                    exps(unit, 0)
                    if u == 1:
                        q_out(p, 1)
                    if u == 3 and not last:
                        q_out(p + 1, 0)
                    for t in range(1, STEPS):
                        exps(unit, t)
                    act.wait_ge(s["pv"], unit * STEPS + STEPS)
                    act.wait_ge(s["norm"], 1 + unit)
                    act.activation(LD[:, :], PV[64:128, :], ACT.Ln).then_inc(s["rd"], 1)
                    act.wait_ge(s["rd"], unit * 2 + 1)
                    act.activation(RD[:, :], LD[:, :], ACT.Exp, scale=-1.0).then_inc(s["rd"], 1)

                inverse_root(0)
                act.wait_ge(s["hT"], b + 1)
                act.activation(HT[:, :], SC[:, 0, :], ACT.Copy).then_inc(s["hTc"], 1)
                q_out(0, 0)
                with act.Fori(0, PAIRS - 1) as p:
                    for u in range(UNITS):
                        unit_acts(p, u, False)
                for u in range(UNITS):
                    unit_acts(PAIRS - 1, u, True)
                act.wait_ge(s["op"], 1 + b + 1)
                act.activation(TA[:, :, :].rearrange("p t d -> p (t d)"), SC[:, 0, :], ACT.Identity, bias=bos[:, 0:1]).then_inc(s["opc"], 1)
                inverse_root(1)
                inverse_root(2)
                act.wait_ge(s["h3T"], b + 1)
                act.activation(HT[:, :], SC[:, 0, :], ACT.Copy).then_inc(s["h3Tc"], 1)
                act.wait_ge(s["qkv"], b + 1)
                act.activation(qkv[:, :, :], SCF.rearrange("p (t n) -> p t n", t=NT)[:, :, 0:QKV], ACT.Copy).then_inc(s["qkvc"], 1)
                act.wait_ge(s["kT"], b + 1)
                for g in range(NG):
                    last = act.activation(KT[32 * g:32 * g + 32, g, :], SC[32 * g:32 * g + 32, 0, :], ACT.Copy)
                last.then_inc(s["kTc"], 1)
                with act.Fori(0, HPG) as j:
                    J = b * HPG + j
                    act.wait_ge(s["ta"], J + 1)
                    act.activation(QTA[:, :], SC[:, 0, :], ACT.Copy).then_inc(s["qta"], 1)
                    act.wait_ge(s["tb"], 1 + J + 1)
                    act.activation(QTB[:, :], SC[:, 0, :], ACT.Copy).then_inc(s["qtb"], 1)
                    n = 0
                    for c in range(NC):
                        for kt in range(4 * c + 4):
                            off, cnt = rows((c, kt))
                            pvi = 4 * c + kt
                            for hh in range(2):
                                act.wait_ge(s["main2"], J * ST2 + n + 1)
                                if pvi >= 2:
                                    act.wait_ge(s["pv2"], J * PV2 + pvi - 1)
                                act.activation(P[:, pvi % 2, 2 * hh:2 * hh + 2, off:CH],
                                               SC[:, n % 2, :].rearrange("p (g q) -> p g q", g=2)[:, :, off:CH],
                                               ACT.Exp, scale=HD ** -0.5).then_inc(s["exp2"], 1)
                                n += 1
                        act.wait_ge(s["pv2"], J * PV2 + pvi + 1)
                        act.wait_ge(s["ovt"], 1 + J * 2 + c)
                        act.activation(OV[:, :], PV[:, :], ACT.Copy).then_inc(s["ov"], 1)
                act.wait_ge(s["aoT"], b + 1)
                act.activation(HT[:, :], SC[:, 0, :], ACT.Copy).then_inc(s["aoTc"], 1)
                inverse_root(3)
                act.wait_ge(s["h4T"], 1 + b + 1)
                act.activation(HT[:, :], SC[:, 0, :], ACT.Copy).then_inc(s["h4Tc"], 1)
                act.wait_ge(s["lg"], b * 2 + 2)
                act.activation(W8[:, :, :], L8[:, :, :], ACT.Exp).then_inc(s["rt"], 1)
                with act.Fori(0, E // 2) as ee:
                    for k in range(2):
                        for t in range(4):
                            act.wait_ge(s["up"], (b * E + ee * 2 + k) * 4 + t + 1)
                            act.activation(SG[:, t % 2, :], SC[:, t % 2, 0:CH], ACT.Silu).then_inc(s["silu"], 1)

        @block.vector
        def _(dve):
            link0 = Chain(dve, s["one"])
            link = link0.link
            dve.memset(KL[:, :].bitcast(F32), 0.0).then_inc(s["const"], 1)
            dve.memset(V1[:, :, :], 1.0).then_inc(s["const"], 1)
            dve.memset(Q2[0][:, :].bitcast(F32), 0.0).then_inc(s["const"], 1)
            dve.memset(Q2[1][:, :].bitcast(F32), 0.0).then_inc(s["const"], 1)
            dve.memset(KT[:, :, :].bitcast(F32), 0.0).then_inc(s["const"], 1)
            dve.memset(QSJ[:, :, :, :].bitcast(F32), 0.0).then_inc(s["const"], 1)
            dve.memset(V2[:, :, :, :], 0.0).then_inc(s["const"], 1)
            dve.memset(M2[:, :, :, :], LOW).then_inc(s["const"], 1)
            dve.wait_ge(s["const"], 8)
            dve.memset(KL[64:65, :].bitcast(F32), 1.0).then_inc(s["const"], 1)
            dve.memset(V2[:, :, :, HD:2 * HD], 1.0).then_inc(s["const"], 1)
            dve.wait_ge(s["csil"], 1)
            for b in range(B):
                last = dve.tensor_copy(cbc[:, b, :], csil[:, b:b + 1].to_broadcast([128, 128]))
            last.then_inc(s["cbc"], 1)
            dve.wait_ge(s["mod"], 1)
            for b in range(B):
                last = dve.tensor_copy(mods[:, b, 0:3, :], MX[:, 0:384].rearrange("p (k d) -> p k d", k=3)) if b == 0 else \
                    dve.tensor_copy(mods[:, b, 0:3, :], PV[:, 0:384].rearrange("p (k d) -> p k d", k=3))
                last = dve.tensor_copy(mods[:, b, 3:6, :], MX[:, 512:896].rearrange("p (k d) -> p k d", k=3)) if b == 0 else \
                    dve.tensor_copy(mods[:, b, 3:6, :], XP[:, 0:384].rearrange("p (k d) -> p k d", k=3))
            link(last)
            for b in range(B):
                for k in (1, 4):
                    link(dve.tensor_scalar(mods[:, b, k, :], mods[:, b, k, :], 1.0, None, ALU.add))
                for k in (2, 5):
                    link(dve.tensor_scalar(gsgn[:, :], mods[:, b, k, :], 0.0, 2.0, ALU.is_ge, ALU.mult))
                    link(dve.scalar_tensor_tensor(out=mods[:, b, k, :], in0=gsgn[:, :], scalar=1.0,
                                                  in1=mods[:, b, k, :], op0=ALU.subtract, op1=ALU.mult))
                    link(dve.tensor_scalar(mods[:, b, k, :], mods[:, b, k, :], 0.25, None, ALU.max))
                    link(dve.scalar_tensor_tensor(out=mods[:, b, k, :], in0=gsgn[:, :], scalar=1.0,
                                                  in1=mods[:, b, k, :], op0=ALU.subtract, op1=ALU.mult))
            dve.wait_ge(s["small"], 16 * 15)
            dve.wait_ge(s["io"], 1)
            dve.wait_ge(s["tri"], 1)
            with dve.Fori(0, B) as b:
                ch = Chain(dve, s["dve"])
                ch.base = b * DVE_STEPS
                link = ch.link

                def tt(o, x, y, op):
                    return dve.tensor_tensor(o, x, y, op)

                def inverse_root(k):
                    dve.wait_ge(s["r0"], b * 8 + 2 * k + 2)
                    link(tt(st[:, 5, :], st[:, 4, :], st[:, 4, :], ALU.mult))
                    link(tt(st[:, 5, :], st[:, 5, :], st[:, 2, :], ALU.mult))
                    link(dve.tensor_scalar(st[:, 5, :], st[:, 5, :], -0.5, 1.5, ALU.mult, ALU.add))
                    link(tt(st[:, 5, :], st[:, 5, :], st[:, 4, :], ALU.mult))

                def mean_square(x, k):
                    link(tt(TB[:, :, :], x, x, ALU.mult))
                    link(dve.tensor_reduce(st[:, 1, :], TB[:, :, :], AX_X, ALU.add))
                    dve.tensor_scalar(st[:, 2, :], st[:, 1, :], 1.0 / D, EPS, ALU.mult, ALU.add).then_inc(s["var"], 1)

                def layer_norm(x, o, k, shift, scale):
                    link(dve.tensor_reduce(st[:, 0, :], x, AX_X, ALU.add))
                    link(dve.tensor_scalar(st[:, 0, :], st[:, 0, :], -1.0 / D, None, ALU.mult))
                    link(tt(o, x, per_token(st[:, 0, :]), ALU.add))
                    mean_square(o, k)
                    inverse_root(k)
                    link(tt(o, o, per_token(st[:, 5, :]), ALU.mult))
                    link(tt(o, o, bc(scale), ALU.mult))
                    return tt(o, o, bc(shift), ALU.add)

                def rms_norm(x, o, k, weight):
                    mean_square(x, k)
                    inverse_root(k)
                    link(tt(o, x, per_token(st[:, 5, :]), ALU.mult))
                    return tt(o, o, bc(weight), ALU.mult)

                dve.wait_ge(s["xld"], b * 16 + 16)
                dve.wait_ge(s["h4T"], 1 + b)
                layer_norm(X[:, :, :], HA[:, :, :], 0, mods[:, b, 0, :], mods[:, b, 1, :]).then_inc(s["h"], 1)
                dve.wait_ge(s["kv"], b + 1)
                link(dve.tensor_scalar(KK[:, :], SC[:, 1, :], bks[:, 0:1], None, ALU.add))
                dve.scalar_tensor_tensor(out=KL[0:64, :], in0=SC[0:64, 1, :], scalar=bks[0:64, 0:1],
                                         in1=KK[0:64, :].bitcast(F32), op0=ALU.add, op1=ALU.subtract)
                tt(V1[:, :, 0:DK], MX[:, 0:CH].rearrange("p (t d) -> p t d", d=DK), bc(bvs[:, :]), ALU.add).then_inc(s["kvx"], 1)

                def split(p, u, first=False):
                    unit = b * (PAIRS * UNITS) + p * UNITS + u
                    dve.wait_ge(s["qf"], b * (2 * PAIRS) + p * 2 + u // 2 + 1)
                    if not first:
                        dve.wait_ge(s["main"], 1 + (unit - 1) * STEPS)
                    src = QF[0:64, :] if u % 2 == 0 else QF[64:128, :]
                    hi = QS[0][0:64, :] if u % 2 == 0 else QS[1][64:128, :]
                    lo = QS[0][64:128, :] if u % 2 == 0 else QS[1][0:64, :]
                    link(dve.tensor_copy(hi, src))
                    dve.tensor_copy(Q2[u % 2][0:64, :], src)
                    tt(lo, src, hi.bitcast(F32), ALU.subtract).then_inc(s["qs"], 1)

                def max_of(p, u, t):
                    unit = b * (PAIRS * UNITS) + p * UNITS + u
                    dve.wait_ge(s["mx"], unit * STEPS + t + 1)
                    if t == 0:
                        dve.wait_ge(s["mt"], 1 + unit)
                    dve.tensor_reduce(MC[:, t:t + 1], MX[:, :], AX_X, ALU.max, negate=True).then_inc(s["mred"], 1)

                def max_out(p, u):
                    unit = b * (PAIRS * UNITS) + p * UNITS + u
                    dve.wait_ge(s["mt"], 1 + unit + 1)
                    dve.wait_ge(s["mdma"], 16 + unit * 16)
                    dve.tensor_copy(MR[:, :], XP[0:STEPS, 0:128]).then_inc(s["mrow"], 1)

                def norm(p, u):
                    unit = b * (PAIRS * UNITS) + p * UNITS + u
                    dve.wait_ge(s["rd"], unit * 2 + 2)
                    link(tt(N1[:, :], PV[64:128, :], RD[:, :], ALU.mult))
                    link(dve.scalar_tensor_tensor(out=N1[:, :], in0=N1[:, :], scalar=2.0, in1=RD[:, :],
                                                  op0=ALU.subtract, op1=ALU.mult))
                    lo = 64 * (u % 2)
                    dve.scalar_tensor_tensor(out=AT[lo:lo + 64, p, (u // 2) * CH:(u // 2) * CH + CH], in0=PV[0:64, :],
                                             scalar=-1.0, in1=N1[:, :], op0=ALU.mult, op1=ALU.mult).then_inc(s["norm"], 1)

                def ahead(p, u):
                    split(p, u)
                    for t in range(STEPS):
                        max_of(p, u, t)
                    max_out(p, u)

                def pair(p, last):
                    for u in range(UNITS):
                        if u < 3:
                            ahead(p, u + 1)
                        elif not last:
                            ahead(p + 1, 0)
                        norm(p, u)

                dve.wait_ge(s["op"], 1 + b)
                split(0, 0, first=True)
                for t in range(STEPS):
                    max_of(0, 0, t)
                max_out(0, 0)
                n0 = ch.n
                with dve.Fori(0, PAIRS - 1) as p:
                    ch.base = b * DVE_STEPS + p * DVE_PAIR
                    pair(p, False)
                    got = ch.n - n0
                assert got == DVE_PAIR, got
                ch.base = b * DVE_STEPS
                ch.n = n0 + (PAIRS - 1) * DVE_PAIR
                pair(PAIRS - 1, True)

                dve.wait_ge(s["opT"], b + 1)
                link(tt(X1[:, :, :], tiles(SC[:, 1, :]), bc(mods[:, b, 2, :]), ALU.mult))
                link(tt(X1[:, :, :], X1[:, :, :], X[:, :, :], ALU.add))
                dve.sem_inc(s["x1"], 1)
                link(layer_norm(X1[:, :, :], H2[:, :, :], 1, mods[:, b, 3, :], mods[:, b, 4, :]))
                rms_norm(H2[:, :, :], HA[:, :, :], 2, lns[:, 0, :]).then_inc(s["h3"], 1)

                dve.wait_ge(s["qkvc"], b + 1)
                nqk = QKV - NG * HD
                half = HD // 2
                for t in range(NT):
                    q3 = qkv[:, t, 0:nqk].rearrange("p (h d) -> p h d", d=HD)
                    r3 = qkr[:, t, :].rearrange("p (h d) -> p h d", d=HD)
                    tt(r3[:, :, 0:half], q3[:, :, half:HD], ropes[:, t, 1, 0:half].unsqueeze(1).to_broadcast([128, nqk // HD, half]), ALU.mult)
                    tt(r3[:, :, half:HD], q3[:, :, 0:half], ropes[:, t, 1, half:HD].unsqueeze(1).to_broadcast([128, nqk // HD, half]), ALU.mult)
                    last = tt(qko[:, t, :].rearrange("p (h d) -> p h d", d=HD), q3, ropes[:, t, 0, :].unsqueeze(1).to_broadcast([128, nqk // HD, HD]), ALU.mult)
                link(last)
                link(tt(qkr[:, :, :], qkr[:, :, :], qko[:, :, :], ALU.add))
                dve.tensor_copy(V2[:, :, :, 0:HD], qkv[:, :, nqk:QKV].rearrange("p t (g d) -> p t g d", g=NG)).then_inc(s["vset"], 1)
                k4 = qkr[:, :, 128:nqk].rearrange("p t (g d) -> p t g d", g=NG)
                link(dve.tensor_copy(KS[:, :, :, 0:8], k4))
                dve.tensor_copy(KS[:, :, :, 8:16], k4)
                tt(KS[:, :, :, 16:24], k4, KS[:, :, :, 0:8].bitcast(F32), ALU.subtract)
                dve.memset(KS[:, :, :, MROW:MROW + 1].bitcast(F32), 1.0).then_inc(s["ks"], 1)
                dve.wait_ge(s["kT"], b + 1)
                plain(dve)
                n0 = ch.n
                with dve.Fori(0, HPG) as j:
                    ch.base = b * DVE_STEPS + j * DVE_J
                    J = b * HPG + j
                    q4 = qkr[:, :, 0:128].rearrange("p t (g j d) -> p j t g d", g=NG, j=HPG)[:, j]
                    dve.wait_ge(s["tb"], 1 + J)
                    plain(dve)
                    link(dve.tensor_copy(QSJ[:, :, :, 0:8], q4))
                    plain(dve)
                    dve.tensor_copy(QSJ[:, :, :, 16:24], q4)
                    dve.memset(QSJ[:, :, :, MROW:MROW + 1].bitcast(F32), 0.0)
                    tt(QSJ[:, :, :, 8:16], q4, QSJ[:, :, :, 0:8].bitcast(F32), ALU.subtract).then_inc(s["qsj"], 1)
                    for t, g, piece, k0, w in pieces():
                        i = item(t, g, piece)
                        dve.wait_ge(s["m2"], J * ITEMS + i + 1)
                        if i >= 8:
                            dve.wait_ge(s["m2red"], 1 + J * ITEMS + i - 7)
                        plain(dve)
                        src = MX[:, (i % 2) * CH:(i % 2) * CH + w]
                        if piece:
                            ins = dve.tensor_tensor_reduce(out=junk[:, i % 8, 0:w], in0=src, in1=tri[:, CH - w:CH], scale=1.0,
                                                           scalar=-3.0e38, op0=ALU.add, op1=ALU.max, accum_out=M2[:, t, g, 0:1])
                        else:
                            ins = dve.tensor_reduce(M2[:, t, g, 1:2], src, AX_X, ALU.max)
                        ins.then_inc(s["m2red"], 1)
                    dve.wait_ge(s["m2red"], 1 + J * ITEMS + ITEMS)
                    dve.tensor_reduce(QSJ[:, :, :, MROW:MROW + 1], M2[:, :, :, :], AX_X, ALU.max, negate=True).then_inc(s["qsm"], 1)
                    for c in range(NC):
                        dve.wait_ge(s["ovt"], 1 + J * 2 + c + 1)
                        x4 = XP[:, :].rearrange("p (t g r) -> p t g r", t=4, g=NG)
                        link(dve.reciprocal(RC[:, :, :], x4[:, :, :, HD]))
                        link(tt(AO[:, 4 * c:4 * c + 4, :].rearrange("p t (g j d) -> p j t g d", g=NG, j=HPG)[:, j],
                                x4[:, :, :, 0:HD], RC[:, :, :].unsqueeze(3).to_broadcast([128, 4, NG, HD]), ALU.mult))
                        dve.sem_inc(s["ao"], 1)
                    got = ch.n - n0
                assert got == DVE_J, got
                ch.base = b * DVE_STEPS
                ch.n = n0 + HPG * DVE_J

                dve.wait_ge(s["wo2"], b + 1)
                link(tt(H2[:, :, :], tiles(SC[:, 1, :]), H2[:, :, :], ALU.add))
                rms_norm(H2[:, :, :], HA[:, :, :], 3, lns[:, 1, :]).then_inc(s["h4"], 1)
                dve.wait_ge(s["lg"], b * 2 + 1)
                link(dve.tensor_copy(L8[:, :, :], XP[:, 0:NT * E].rearrange("p (t e) -> p t e", e=E)))
                plain(dve)
                for t in range(NT):
                    last = dve.max(T8[:, t, :], L8[:, t, :])
                link(last)
                plain(dve)
                for t in range(NT):
                    last = dve.max_index(I8[:, t, :], T8[:, t, :], L8[:, t, :])
                link(last)
                link(tt(L8[:, :, :], L8[:, :, :], T8[:, :, 0:1].to_broadcast([128, NT, E]), ALU.subtract))
                dve.sem_inc(s["lg"], 1)
                link(dve.tensor_copy(IF[:, :, :], I8[:, :, 0:2]))
                link(tt(WF[:, :, :], bc(io8[:, :]), IF[:, :, 0:1].to_broadcast([128, NT, E]), ALU.is_equal))
                link(tt(T8[:, :, :], bc(io8[:, :]), IF[:, :, 1:2].to_broadcast([128, NT, E]), ALU.is_equal))
                link(tt(WF[:, :, :], WF[:, :, :], T8[:, :, :], ALU.add))
                dve.wait_ge(s["rt"], b + 1)
                link(tt(WF[:, :, :], WF[:, :, :], W8[:, :, :], ALU.mult))
                link(dve.tensor_reduce(st[:, 6, :], WF[:, :, :], AX_X, ALU.add))
                link(dve.reciprocal(st[:, 7, :], st[:, 6, :]))
                link(tt(WF[:, :, :], WF[:, :, :], per_token(st[:, 7, :], E), ALU.mult))
                link(dve.memset(ACC[:, :, :], 0.0))
                dve.wait_ge(s["out"], 16 + b * 16)
                plain(dve)
                with dve.Fori(0, E // 2) as ee:
                    for k in range(2):
                        n = b * E + ee * 2 + k

                        def gated(t):
                            dve.wait_ge(s["silu"], n * 4 + t + 1)
                            tt(G[:, t // 2, t % 2, :], SG[:, t % 2, :], SC[:, t % 2, CH:2 * CH], ALU.mult).then_inc(s["g"], 1)

                        def accumulate(c):
                            if c == 0:
                                dve.wait_ge(s["down"], n + 1)
                            else:
                                dve.wait_ge(s["slot"], n + 3)
                            tt(TA[:, 4 * c:4 * c + 4, :], tiles(MX[:, c * CH:(c + 1) * CH]),
                               WF[:, 4 * c:4 * c + 4, bass.ds(ee * 2 + k, 1)].to_broadcast([128, 4, D]), ALU.mult).then_inc(s["accfree"], 1)
                            dve.wait_ge(s["accfree"], n * 2 + c + 3)
                            tt(ACC[:, 4 * c:4 * c + 4, :], ACC[:, 4 * c:4 * c + 4, :], TA[:, 4 * c:4 * c + 4, :], ALU.add).then_inc(s["mods"], 1)

                        gated(0)
                        gated(1)
                        gated(2)
                        gated(3)
                        dve.wait_ge(s["mods"], 1 + n * 2)
                        accumulate(0)
                        accumulate(1)
                dve.wait_ge(s["mods"], 1 + b * (2 * E) + 2 * E)
                link(tt(TA[:, :, :], ACC[:, :, :], H2[:, :, :], ALU.add))
                link(tt(TA[:, :, :], TA[:, :, :], bc(mods[:, b, 5, :]), ALU.mult))
                tt(TA[:, :, :], TA[:, :, :], X1[:, :, :], ALU.add).then_inc(s["y"], 1)
                assert ch.n == DVE_STEPS, ch.n

        @block.tensor
        def _(pe):
            mm = pe.matmul
            pe.wait_ge(s["idn"], 3)
            pe.wait_ge(s["wmodld"], 32)
            pe.wait_ge(s["const"], 10)
            pe.wait_ge(s["cbc"], 1)
            for o, b, c in ((MX[:, 0:384], 0, 0), (MX[:, 512:896], 0, 1), (PV[:, 0:384], 1, 0), (XP[:, 0:384], 1, 1)):
                last = mm(o, cbc[:, b, :], wmods[:, c * 384:(c + 1) * 384], start=True, stop=True)
            last.then_inc(s["mod"], 1)
            pe.wait_ge(s["small"], 16 * 15)
            pe.wait_ge(s["one"], 21)
            with pe.Fori(0, B) as b:
                def transposes(src, half):
                    for t in range(NT):
                        last = pe.transpose(SC[:, half, t * 128:t * 128 + 128], src[:, t, :], ident[:, :])
                    return last

                pe.wait_ge(s["h"], b + 1)
                transposes(HA, 0).then_inc(s["hT"], 1)
                pe.wait_ge(s["hTc"], b + 1)
                for c in range(NC):
                    mm(SC[:, 1, c * CH:(c + 1) * CH], wk2[:, :], HT[:, c * CH:(c + 1) * CH], start=True, stop=True)
                for t in range(NT):
                    last = mm(MX[:, t * DK:(t + 1) * DK], HT[:, t * 128:(t + 1) * 128], wvs[:, :], start=True, stop=True)
                last.then_inc(s["kv"], 1)

                def q_proj(p, c):
                    pe.wait_ge(s["wqld"], (b * PAIRS + p) * 16 + 16)
                    pe.wait_ge(s["mrow"], 1 + (b * (2 * PAIRS) + p * 2 + c) * 2)
                    mm(XP[:, :], wqs[:, :], HT[:, c * CH:(c + 1) * CH], start=True, stop=True).then_inc(s["q"], 1)

                def max_pass(p, u, t):
                    unit = b * (PAIRS * UNITS) + p * UNITS + u
                    if t == 0:
                        pe.wait_ge(s["qs"], 1 + unit + 1)
                    pe.wait_ge(s["mred"], 1 + unit * STEPS + t)
                    q = QS[u % 2][:, t * 128:(t + 1) * 128]
                    mm(MX[:, 0:CH], q, KK[:, 0:CH], start=True, stop=True)
                    mm(MX[:, CH:S], q, KK[:, CH:S], start=True, stop=True).then_inc(s["mx"], 1)

                def max_turn(p, u):
                    unit = b * (PAIRS * UNITS) + p * UNITS + u
                    pe.wait_ge(s["mred"], 1 + unit * STEPS + STEPS)
                    pe.wait_ge(s["qf"], b * (2 * PAIRS) + p * 2 + u // 2 + 1)
                    pe.wait_ge(s["mrow"], 1 + unit)
                    pe.transpose(XP[0:STEPS, 0:128], MC[:, :], ident[:, :]).then_inc(s["mt"], 1)

                def scores(unit, u, t):
                    if t >= 2:
                        pe.wait_ge(s["exp"], unit * STEPS + t - 1)
                    for k in range(2):
                        kt = 2 * t + k
                        mm(SC[:, t % 2, k * CH:(k + 1) * CH], KK[:, kt * 128:(kt + 1) * 128], QS[u % 2][:, :], start=True, stop=False)
                    if t == 0:
                        pe.wait_ge(s["mdma"], 16 + unit * 16 + 16)
                    for k in range(2):
                        kt = 2 * t + k
                        last = mm(SC[:, t % 2, k * CH:(k + 1) * CH], KL[:, kt * 128:(kt + 1) * 128], Q2[u % 2][:, :], start=False, stop=True)
                    last.then_inc(s["main"], 1)

                def weigh(unit, t):
                    pe.wait_ge(s["exp"], unit * STEPS + t + 1)
                    if t == 0:
                        pe.wait_ge(s["norm"], 1 + unit)
                    for k in range(2):
                        kt = 2 * t + k
                        last = mm(PV[:, :], V1[:, kt, :], P[:, t % 2, k, :], start=(kt == 0), stop=(kt == NT - 1))
                    last.then_inc(s["pv"], 1)

                def unit_mms(p, u, last):
                    unit = b * (PAIRS * UNITS) + p * UNITS + u
                    np_, nu = (p, u + 1) if u < 3 else (p + 1, 0)
                    more = not (last and u == 3)
                    scores(unit, u, 0)
                    if more and nu % 2 == 0:
                        q_proj(np_, nu // 2)
                    scores(unit, u, 1)
                    weigh(unit, 0)
                    if more:
                        max_pass(np_, nu, 0)
                    scores(unit, u, 2)
                    if more:
                        max_pass(np_, nu, 1)
                    weigh(unit, 1)
                    if more:
                        max_pass(np_, nu, 2)
                    scores(unit, u, 3)
                    if more:
                        max_pass(np_, nu, 3)
                    weigh(unit, 2)
                    if more:
                        max_turn(np_, nu)
                    weigh(unit, 3)

                q_proj(0, 0)
                pe.wait_ge(s["kvx"], b + 1)
                for t in range(STEPS):
                    max_pass(0, 0, t)
                max_turn(0, 0)
                with pe.Fori(0, PAIRS - 1) as p:
                    for u in range(UNITS):
                        unit_mms(p, u, False)
                for u in range(UNITS):
                    unit_mms(PAIRS - 1, u, True)
                pe.wait_ge(s["norm"], 1 + b * (PAIRS * UNITS) + PAIRS * UNITS)
                for c in range(NC):
                    for p in range(PAIRS):
                        last = mm(SC[:, 0, c * CH:(c + 1) * CH], wos[:, p, :], AT[:, p, c * CH:(c + 1) * CH],
                                  start=(p == 0), stop=(p == PAIRS - 1))
                last.then_inc(s["op"], 1)
                pe.wait_ge(s["opc"], b + 1)
                transposes(TA, 1).then_inc(s["opT"], 1)
                pe.wait_ge(s["h3"], b + 1)
                transposes(HA, 0).then_inc(s["h3T"], 1)
                pe.wait_ge(s["h3Tc"], b + 1)
                for t in range(NT):
                    last = mm(SCF[:, t * 256:t * 256 + QKV], HT[:, t * 128:(t + 1) * 128], WQKVT[:, 0:QKV], start=True, stop=True)
                last.then_inc(s["qkv"], 1)
                pe.wait_ge(s["ks"], b + 1)
                pe.wait_ge(s["qkvc"], b + 1)

                def turn_stack():
                    for t in range(NT):
                        last = pe.transpose(SC[:, 0, t * 128:t * 128 + 128], QSJ[:, t, :, :].rearrange("p g r -> p (g r)").bitcast(F32), ident[:, :])
                    return last

                turn_stack().then_inc(s["kT"], 1)
                pe.wait_ge(s["kTc"], b + 1)
                pe.wait_ge(s["vset"], b + 1)
                plain(pe)
                with pe.Fori(0, HPG) as j:
                    J = b * HPG + j
                    pe.wait_ge(s["qsj"], J + 1)
                    turn_stack().then_inc(s["ta"], 1)
                    pe.wait_ge(s["qta"], J + 1)
                    for t, g, piece, k0, w in pieces():
                        i = item(t, g, piece)
                        pe.wait_ge(s["m2red"], 1 + J * ITEMS + max(0, i - 1))
                        mm(MX[:, (i % 2) * CH:(i % 2) * CH + w], QTA[:, t * 128:(t + 1) * 128], KT[:, g, k0:k0 + w],
                           start=True, stop=True).then_inc(s["m2"], 1)
                    pe.wait_ge(s["qsm"], J + 1)
                    turn_stack().then_inc(s["tb"], 1)
                    pe.wait_ge(s["qtb"], J + 1)

                    def weigh2(c, kt):
                        off, cnt = rows((c, kt))
                        pvi = 4 * c + kt
                        pe.wait_ge(s["exp2"], J * ST2 + (8 if c else 0) + 2 * kt + 2)
                        if kt >= 4 * c:
                            pe.wait_ge(s["tri2"], J * 16 + 8 * c + 2 * (kt - 4 * c) + 2)
                        if kt == 0:
                            pe.wait_ge(s["ov"], 1 + J * 2 + c)
                        for g in range(NG):
                            last = mm(PV[32 * g:32 * g + 32, off:CH], V2[:, kt, g, :], P[:, pvi % 2, g, off:CH],
                                      start=(kt == 0), stop=(kt == 4 * c + 3))
                        last.then_inc(s["pv2"], 1)

                    def turn_out(c):
                        pe.wait_ge(s["ov"], 1 + J * 2 + c + 1)
                        pe.wait_ge(s["ao"], 1 + J * 2 + c)
                        for t in range(4):
                            last = pe.transpose(XP[:, t * 128:(t + 1) * 128], OV[:, t * 128:(t + 1) * 128], ident[:, :])
                        last.then_inc(s["ovt"], 1)

                    n = 0
                    for c in range(NC):
                        for kt in range(4 * c + 4):
                            off, cnt = rows((c, kt))
                            for hh in range(2):
                                if n >= 2:
                                    pe.wait_ge(s["exp2"], J * ST2 + n - 1)
                                for g in (2 * hh, 2 * hh + 1):
                                    last = mm(SC[:, n % 2, (g % 2) * CH + off:(g % 2) * CH + CH], KT[:, g, kt * 128:(kt + 1) * 128],
                                              QTB[:, c * CH + off:(c + 1) * CH], start=True, stop=True)
                                last.then_inc(s["main2"], 1)
                                n += 1
                            if kt > 0:
                                weigh2(c, kt - 1)
                            if c == 1 and kt == 2:
                                turn_out(0)
                        weigh2(c, 4 * c + 3)
                    turn_out(1)
                pe.wait_ge(s["ao"], 1 + b * (2 * HPG) + 2 * HPG)
                transposes(AO, 0).then_inc(s["aoT"], 1)
                pe.wait_ge(s["aoTc"], b + 1)
                for t in range(NT):
                    last = mm(SC[:, 1, t * 128:(t + 1) * 128], HT[:, t * 128:(t + 1) * 128], WOT[:, :], start=True, stop=True)
                last.then_inc(s["wo2"], 1)
                pe.wait_ge(s["h4"], b + 1)
                transposes(HA, 0).then_inc(s["h4T"], 1)
                pe.wait_ge(s["h4Tc"], b + 1)
                for t in range(NT):
                    last = mm(XP[:, t * E:(t + 1) * E], HT[:, t * 128:(t + 1) * 128], gates[:, :], start=True, stop=True)
                last.then_inc(s["lg"], 1)
                with pe.Fori(0, E // 2) as ee:
                    for k in range(2):
                        n = b * E + ee * 2 + k

                        def up(t):
                            if t == 0:
                                pe.wait_ge(s["wcopy"], n + 1)
                            if t >= 2:
                                pe.wait_ge(s["g"], n * 4 + t - 1)
                            c, f = t // 2, t % 2
                            mm(SC[:, t % 2, 0:CH], W13S[k][:, f * 128:(f + 1) * 128], HT[:, c * CH:(c + 1) * CH], start=True, stop=True)
                            mm(SC[:, t % 2, CH:2 * CH], W13S[k][:, FFN + f * 128:FFN + (f + 1) * 128], HT[:, c * CH:(c + 1) * CH],
                               start=True, stop=True).then_inc(s["up"], 1)

                        def down(c):
                            pe.wait_ge(s["g"], n * 4 + 2 * c + 2)
                            pe.wait_ge(s["accfree"], n * 2 + c + 1)
                            for t in range(4):
                                for f in range(2):
                                    last = mm(MX[:, c * CH + t * 128:c * CH + (t + 1) * 128], G[:, c, f, t * 128:(t + 1) * 128],
                                              W2S[k][:, f * D:(f + 1) * D], start=(f == 0), stop=(f == 1))
                            last.then_inc(s["down"] if c == 0 else s["slot"], 1)

                        up(0)
                        up(1)
                        up(2)
                        down(0)
                        up(3)
                        down(1)


_INS = ["L0_attn_x", "L0_attn_Wq", "L0_attn_bq", "L0_attn_Wk", "L0_attn_bk", "L0_attn_Wv", "L0_attn_bv", "L0_attn_Wo",
        "L0_attn_bo", "L0_ffn_ln1_w", "L0_ffn_ln2_w", "L0_ffn_wqkv", "L0_ffn_wo", "L0_ffn_gate_w", "L0_ffn_w13",
        "L0_ffn_w2", "L0_c", "L0_wmod"]


def kernel(**inputs):
    import numpy as np
    import concourse.bacc as bacc
    from concourse.bass_utils import run_bass_kernel_spmd

    nc = bacc.Bacc("TRN2", target_bir_lowering=False, num_devices=1)
    lay = {
        "L0_attn_bq": lambda a: a.reshape(PAIRS, 128).T,
        "L0_ffn_wqkv": lambda a: a.T,
        "L0_ffn_wo": lambda a: a.T,
        "L0_ffn_gate_w": lambda a: a.T,
        "L0_ffn_w13": lambda a: a.transpose(2, 0, 1),
        "L0_ffn_w2": lambda a: a.reshape(E, D, 2, 128).transpose(3, 0, 2, 1).reshape(128, E, 2 * D),
        "L0_c": lambda a: a.T,
    }
    arrays, args = {}, []
    for name in _INS:
        a = np.asarray(inputs[name])
        a = np.ascontiguousarray(lay[name](a) if name in lay else a)
        arrays["in_" + name] = a
        args.append(nc.dram_tensor("in_" + name, a.shape, mybir.dt.from_np(a.dtype), kind="ExternalInput").ap())
    inv = (np.float32(1.0) / np.float32(10000.0) ** (np.arange(0, HD, 2, dtype=np.float32) / np.float32(HD))).astype(np.float32)
    ang = np.arange(S, dtype=np.float32)[:, None] * inv[None, :]
    cos, sin = np.cos(ang), np.sin(ang)
    rope = np.stack([np.concatenate([cos, cos], 1), np.concatenate([-sin, sin], 1)], 1).astype(np.float32)
    arrays["rope"] = rope
    args.append(nc.dram_tensor("rope", rope.shape, F32, kind="ExternalInput").ap())
    out = nc.dram_tensor("out_0", (B, S, D), F32, kind="ExternalOutput").ap()
    build(nc, *args, out)
    r = run_bass_kernel_spmd(nc, [arrays], core_ids=[0])
    return r.results[0]["out_0"]
```

```python
from contextlib import ExitStack

import concourse.bass as bass
from concourse import mybir

F32 = mybir.dt.float32
F32R = mybir.dt.float32r
ALU = mybir.AluOpType
ACT = mybir.ActivationFunctionType
AX_X = mybir.AxisListType.X

B, S, D = 2, 1024, 128
NT = S // 128
NC = 2
CH = S // NC
H, DK = 16, 64
PAIRS = H // 2
UNITS = 4
STEPS = 4
NG, HPG, HD = 4, 4, 8
NH2 = NG * HPG
QKV = (NH2 + 2 * NG) * HD
ROWS = 32
MROW = 24
ITEMS = 48
ST2 = 24
PV2 = 12
E, FFN = 8, 256
EPS = 1e-5
LOW = -1.0e30
DVE_STEPS = 175
DVE_PAIR = 12
DVE_J = 5


class Chain:

    def __init__(self, eng, sem):
        self.eng, self.sem, self.n, self.base = eng, sem, 0, 0

    def link(self, ins):
        self.n += 1
        ins.then_inc(self.sem, 1)
        self.eng.wait_ge(self.sem, self.base + self.n)


def rows(n):
    c, kt = n
    off = max(0, kt * 128 - c * CH)
    return off, CH - off


def item(t, g, piece):
    return 4 * t + g if t < 4 else 16 + 8 * (t - 4) + 2 * g + piece


def pieces(step):
    every = []
    for t in range(NT):
        for g in range(NG):
            if t >= 4:
                every.append((t, g, 0, 0, CH))
            every.append((t, g, 1, CH * (t // 4), (t % 4 + 1) * 128))
    return every if step is None else every[5 * (step - 2):5 * (step - 1)] if step >= 2 else []


def build(nc, a_x, Wq, bq, Wk, bk, Wv, bv, Wo, bo, ln1, ln2, wqkv, wo, gate, w13, w2, cin, wmod, rope, out):
    with ExitStack() as ctx:
        def sb(name, shape, dt=F32):
            return ctx.enter_context(nc.sbuf_tensor(name, shape, dt))

        def ps(name, shape):
            return ctx.enter_context(nc.psum_tensor(name, shape, F32))

        def sem(name):
            return ctx.enter_context(nc.semaphore(name))

        SC = ps("SC", [128, 2, 1024])
        SCF = SC[:, :, :].rearrange("p a b -> p (a b)")
        MX = ps("MX", [128, 1024])
        PV = ps("PV", [128, CH])
        XP = ps("XP", [128, CH])

        ident = sb("ident", [128, 128])
        tri = sb("tri", [128, CH])
        wk2 = sb("wk2", [128, 128])
        wvs = sb("wvs", [128, DK])
        wos = sb("wos", [128, PAIRS, D])
        bqs = sb("bqs", [128, PAIRS])
        bks = sb("bks", [128, 1])
        bvs = sb("bvs", [128, DK])
        bos = sb("bos", [128, 1])
        lns = sb("lns", [128, 2, D])
        cs = sb("cs", [128, B])
        csil = sb("csil", [128, B])
        cbc = sb("cbc", [128, B, 128])
        wmods = sb("wmods", [128, 6 * D])
        mods = sb("mods", [128, B, 6, D])
        gsgn = sb("gsgn", [128, D])
        gates = sb("gates", [128, E])
        ropes = sb("ropes", [128, NT, 2, HD])
        BIG = sb("BIG", [128, PAIRS * S])
        AT = BIG[:, :].rearrange("p (j n) -> p j n", j=PAIRS)
        W13T = sb("W13T", [128, E, 2 * FFN])
        W2T = sb("W2T", [128, E, 2 * D])
        WQKVT = sb("WQKVT", [128, QKV])
        WOT = sb("WOT", [128, D])

        X = sb("X", [128, NT, D])
        X1 = sb("X1", [128, NT, D])
        HA = sb("HA", [128, NT, D])
        H2 = sb("H2", [128, NT, D])
        TA = sb("TA", [128, NT, D])
        TB = sb("TB", [128, NT, D])
        HT = sb("HT", [128, S])
        st = sb("st", [128, 8, NT])
        wqs = sb("wqs", [128, 128])
        KK = sb("KK", [128, S], F32R)
        KL = sb("KL", [128, S], F32R)
        V1 = sb("V1", [128, NT, 128])
        QF = sb("QF", [128, CH])
        QS = [sb(f"QS{i}", [128, CH], F32R) for i in range(2)]
        Q2 = [sb(f"Q2{i}", [128, CH], F32R) for i in range(2)]
        MC = sb("MC", [128, STEPS])
        MR = sb("MR", [STEPS, 128], F32R)
        P = sb("P", [128, 2, NG, CH])
        OE = sb("OE", [128, CH])
        LD = sb("LD", [128, CH])
        RD = sb("RD", [128, CH])
        QSJ = sb("QSJ", [128, NT, NG, ROWS], F32R)
        KT = sb("KT", [128, NG, S], F32R)
        QTA = sb("QTA", [128, S], F32R)
        QTB = sb("QTB", [128, HPG, S], F32R)
        V2 = sb("V2", [128, NT, NG, ROWS])
        M2 = sb("M2", [128, NT, NG, 2])
        RC = sb("RC", [128, 4, NG])
        L8 = sb("L8", [128, NT, E])
        T8 = sb("T8", [128, NT, 8])
        I8 = sb("I8", [128, NT, 8], mybir.dt.uint32)
        IF = sb("IF", [128, NT, 2])
        io8 = sb("io8", [128, E])
        WF = sb("WF", [128, NT, E])
        W8 = sb("W8", [128, NT, E])
        W13S = [sb(f"W13S{i}", [128, 2 * FFN]) for i in range(2)]
        W2S = [sb(f"W2S{i}", [128, 2 * D]) for i in range(2)]
        AO = TB
        KS = QSJ
        SG = P[:, 0, 0:2, :]
        G = P[:, 1, :, :].rearrange("p (c f) q -> p c f q", c=NC)
        ACC = BIG[:, 0:S].rearrange("p (t d) -> p t d", t=NT)
        OV = BIG[:, S:S + CH]
        junk = BIG[:, 2 * S:4 * S].rearrange("p (n q) -> p n q", n=4)
        NQK = QKV - NG * HD
        qkv = BIG[:, 4 * S:4 * S + NT * QKV].rearrange("p (t n) -> p t n", t=NT)
        qkr = BIG[:, 4 * S + NT * QKV:4 * S + NT * (QKV + NQK)].rearrange("p (t n) -> p t n", t=NT)
        qko = BIG[:, 4 * S + NT * (QKV + NQK):8 * S].rearrange("p (t n) -> p t n", t=NT)

        names = """small rawld wmodld idn tri io const one turn csil cbc mod mods xld wqld dve var r0
            h hT hTc kv kvx q qf qs mx mred mt mrow mdma main exp pv pve rd norm a1 op opc opT x1 h3 h3T h3Tc qkv
            qkvc ks kT kTc vset qsj ta qta m2 m2red qsm tb qtb main2 exp2 tri2 pv2 ovc ov ovt ao aoT aoTc wo2 h4 h4T
            h4Tc lg rt slot wcopy up silu g down accfree y out""".split()
        s = {n: sem("s_" + n) for n in names}
        block = ctx.enter_context(nc.Block())

        def bc(ap, n=NT):
            return ap.unsqueeze(1).to_broadcast([128, n, ap.shape[-1]])

        def per_token(ap, n=D):
            return ap.unsqueeze(2).to_broadcast([128, ap.shape[1], n])

        def tiles(ap):
            return ap.rearrange("p (t d) -> p t d", d=128)

        def plain(eng):
            eng.sem_inc(s["turn"], 1)

        STARTED = {n: 1 for n in "x1 q h4T op mt mrow mred qs pve norm tb m2red ovt ov ao mods main".split()} | {"mdma": 16, "out": 16}

        @block.sync
        def _(sp):
            for n, turn in STARTED.items():
                sp.sem_inc(s[n], turn)
            sp.dma_start(cs[:, :], cin).then_inc(s["wmodld"], 16)
            sp.dma_start(wmods[:, :], wmod).then_inc(s["wmodld"], 16)
            small = [
                (wk2[:, 0:DK], Wk), (wk2[:, DK:128], Wk), (wvs[:, :], Wv),
                (wos[:, :, :], Wo.rearrange("(j p) d -> p j d", p=128)),
                (bqs[:, :], bq),
                (bks[0:64, :], bk.rearrange("(p a) -> p a", a=1)), (bks[64:128, :], bk.rearrange("(p a) -> p a", a=1)),
                (bvs[:, :], bv.partition_broadcast(128)), (bos[:, :], bo.rearrange("(p a) -> p a", a=1)),
                (lns[:, 0, :], ln1.partition_broadcast(128)), (lns[:, 1, :], ln2.partition_broadcast(128)),
                (gates[:, :], gate), (WQKVT[:, :], wqkv), (WOT[:, :], wo),
                (ropes[:, :, :, :], rope.rearrange("(t p) k d -> p t k d", p=128)),
            ]
            for dst, src in small:
                sp.dma_start(dst, src).then_inc(s["small"], 16)
            sp.dma_start(W13T[:, :, :], w13).then_inc(s["rawld"], 16)
            sp.dma_start(W2T[:, :, :], w2).then_inc(s["rawld"], 16)
            with sp.Fori(0, B) as b:
                sp.wait_ge(s["x1"], 1 + b)
                sp.dma_start(X[:, :, :], a_x[b].rearrange("(t p) d -> p t d", p=128)).then_inc(s["xld"], 16)
                sp.wait_ge(s["q"], 1 + b * (2 * PAIRS))
                sp.dma_start(wqs[:, :], Wq[:, 0:128]).then_inc(s["wqld"], 16)

                def max_row(unit, q2):
                    sp.wait_ge(s["mrow"], 1 + unit + 1)
                    sp.dma_start(q2[64:65, :].bitcast(F32), MR[:, :].bitcast(F32)).then_inc(s["mdma"], 16)

                def pair_rows(p, last):
                    unit = b * (PAIRS * UNITS) + p * UNITS
                    max_row(unit + 1, Q2[1])
                    if not last:
                        sp.wait_ge(s["q"], 1 + b * (2 * PAIRS) + p * 2 + 2)
                        sp.dma_start(wqs[:, :], Wq[:, bass.ds(p * 128 + 128, 128)]).then_inc(s["wqld"], 16)
                    max_row(unit + 2, Q2[0])
                    max_row(unit + 3, Q2[1])
                    if not last:
                        max_row(unit + 4, Q2[0])

                max_row(b * (PAIRS * UNITS), Q2[0])
                with sp.Fori(0, PAIRS - 1) as p:
                    pair_rows(p, False)
                pair_rows(PAIRS - 1, True)
                sp.wait_ge(s["y"], b + 1)
                sp.dma_start(out[b].rearrange("(t p) d -> p t d", p=128), TA[:, :, :]).then_inc(s["out"], 16)
            sp.wait_ge(s["out"], 16 + 16 * B)

        @block.gpsimd
        def _(pool):
            pool.memset(ident[:, :], 0.0).then_inc(s["idn"], 1)
            pool.memset(tri[:, :], 0.0).then_inc(s["idn"], 1)
            pool.wait_ge(s["idn"], 2)
            pool.affine_select(out=ident[:, :], in_=ident[:, :], compare_op=ALU.not_equal, fill=1.0, base=0,
                               pattern=[[-1, 128]], channel_multiplier=1).then_inc(s["idn"], 1)
            pool.affine_select(out=tri[:, CH - 128:CH], in_=tri[:, CH - 128:CH], compare_op=ALU.is_ge, fill=LOW,
                               base=0, pattern=[[-1, 128]], channel_multiplier=1).then_inc(s["tri"], 1)
            pool.iota(io8[:, :], pattern=[[1, E]], base=0, channel_multiplier=0,
                      allow_small_or_imprecise_dtypes=True).then_inc(s["io"], 1)
            pool.memset(W13S[0][:, 0:1], 0.0).then_inc(s["slot"], 2)
            pool.memset(W13S[1][:, 0:1], 0.0).then_inc(s["accfree"], 2)
            pool.wait_ge(s["slot"], 2)
            pool.wait_ge(s["accfree"], 2)
            pool.wait_ge(s["rawld"], 32)
            with pool.Fori(0, B) as b:
                with pool.Fori(0, HPG) as j:
                    n = 0
                    for c in range(NC):
                        for kt in range(4 * c, 4 * c + 4):
                            stp = (8 if c else 0) + 2 * kt
                            off, _ = rows((c, kt))
                            for hh in range(2):
                                pool.wait_ge(s["exp2"], (b * HPG + j) * ST2 + stp + hh + 1)
                                plain(pool)
                                blk = P[:, (4 * c + kt) % 2, 2 * hh:2 * hh + 2, off:off + 128]
                                pool.affine_select(out=blk, in_=blk, compare_op=ALU.is_ge, fill=0.0, base=0,
                                                   pattern=[[0, 2], [1, 128]], channel_multiplier=-1).then_inc(s["tri2"], 1)
                                n += 1
                with pool.Fori(0, E // 2) as ee:
                    for k in range(2):
                        pool.wait_ge(s["slot"], b * E + ee * 2 + k + 1)
                        plain(pool)
                        pool.tensor_copy(W13S[k][:, :], W13T[:, ee * 2 + k, :])
                        pool.tensor_copy(W2S[k][:, :], W2T[:, ee * 2 + k, :]).then_inc(s["wcopy"], 1)

        @block.scalar
        def _(act):
            act.wait_ge(s["wmodld"], 32)
            act.activation(csil[:, :], cs[:, :], ACT.Silu).then_inc(s["csil"], 1)
            act.wait_ge(s["small"], 16 * 15)
            with act.Fori(0, B) as b:
                act.preload_act_table_set("natural_log_exp_and_others")
                def inverse_root(k):
                    act.wait_ge(s["var"], b * 4 + k + 1)
                    act.activation(st[:, 3, :], st[:, 2, :], ACT.Ln).then_inc(s["r0"], 1)
                    act.wait_ge(s["r0"], b * 8 + 2 * k + 1)
                    act.activation(st[:, 4, :], st[:, 3, :], ACT.Exp, scale=-0.5).then_inc(s["r0"], 1)

                def exps(unit, t):
                    act.wait_ge(s["main"], 1 + unit * STEPS + t + 1)
                    if t >= 2:
                        act.wait_ge(s["pv"], unit * STEPS + t - 1)
                    act.activation(P[:, t % 2, 0:2, :].rearrange("p a b -> p (a b)"), SC[:, t % 2, :], ACT.Exp,
                                   scale=DK ** -0.5).then_inc(s["exp"], 1)

                def q_out(p, c):
                    act.wait_ge(s["q"], 1 + b * (2 * PAIRS) + p * 2 + c + 1)
                    act.wait_ge(s["qs"], 1 + (b * (2 * PAIRS) + p * 2 + c) * 2)
                    act.activation(QF[:, :], XP[:, :], ACT.Identity, bias=bqs[:, bass.ds(p, 1)]).then_inc(s["qf"], 1)

                def unit_acts(p, u, last):
                    unit = b * (PAIRS * UNITS) + p * UNITS + u
                    exps(unit, 1)
                    if u == 0:
                        q_out(p, 1)
                    if u == 2 and not last:
                        q_out(p + 1, 0)
                    exps(unit, 2)
                    exps(unit, 3)
                    if not (last and u == 3):
                        exps(unit + 1, 0)
                    act.wait_ge(s["pv"], unit * STEPS + STEPS)
                    act.wait_ge(s["norm"], 1 + unit)
                    act.activation(OE[:, :], PV[:, :], ACT.Copy).then_inc(s["pve"], 1)
                    act.wait_ge(s["pve"], 1 + unit + 1)
                    act.activation(LD[64:128, :], OE[64:128, :], ACT.Ln).then_inc(s["rd"], 1)
                    act.wait_ge(s["rd"], unit * 2 + 1)
                    act.activation(RD[64:128, :], LD[64:128, :], ACT.Exp, scale=-1.0).then_inc(s["rd"], 1)

                inverse_root(0)
                act.wait_ge(s["hT"], b + 1)
                act.activation(HT[:, :], SC[:, 0, :], ACT.Copy).then_inc(s["hTc"], 1)
                q_out(0, 0)
                exps(b * (PAIRS * UNITS), 0)
                with act.Fori(0, PAIRS - 1) as p:
                    for u in range(UNITS):
                        unit_acts(p, u, False)
                for u in range(UNITS):
                    unit_acts(PAIRS - 1, u, True)
                act.wait_ge(s["op"], 1 + b + 1)
                act.activation(TA[:, :, :].rearrange("p t d -> p (t d)"), SC[:, 0, :], ACT.Identity, bias=bos[:, 0:1]).then_inc(s["opc"], 1)
                inverse_root(1)
                inverse_root(2)
                act.wait_ge(s["h3T"], b + 1)
                act.activation(HT[:, :], SC[:, 0, :], ACT.Copy).then_inc(s["h3Tc"], 1)
                act.wait_ge(s["qkv"], b + 1)
                act.activation(qkv[:, :, :], SCF.rearrange("p (t n) -> p t n", t=NT)[:, :, 0:QKV], ACT.Copy).then_inc(s["qkvc"], 1)
                act.wait_ge(s["kT"], b + 1)
                for g in range(NG):
                    last = act.activation(KT[32 * g:32 * g + 32, g, :], SC[32 * g:32 * g + 32, 0, :], ACT.Copy)
                last.then_inc(s["kTc"], 1)

                def q_turned(J):
                    act.wait_ge(s["ta"], J + 1)
                    act.activation(QTA[:, :], MX[:, :], ACT.Copy).then_inc(s["qta"], 1)

                def q_with_max(j):
                    act.wait_ge(s["tb"], 2 + b * HPG + j)
                    act.activation(QTB[:, j, :], MX[:, :], ACT.Copy).then_inc(s["qtb"], 1)

                def heads_of(j, last):
                    J = b * HPG + j
                    n = 0
                    for c in range(NC):
                        for kt in range(4 * c + 4):
                            off, cnt = rows((c, kt))
                            pvi = 4 * c + kt
                            for hh in range(2):
                                act.wait_ge(s["main2"], J * ST2 + n + 1)
                                if pvi >= 2:
                                    act.wait_ge(s["pv2"], J * PV2 + pvi - 1)
                                act.activation(P[:, pvi % 2, 2 * hh:2 * hh + 2, off:CH],
                                               SC[:, n % 2, :].rearrange("p (g q) -> p g q", g=2)[:, :, off:CH],
                                               ACT.Exp, scale=HD ** -0.5).then_inc(s["exp2"], 1)
                                n += 1
                            if pvi == 1 and c == 0 and not last:
                                q_turned(J + 1)
                        act.wait_ge(s["pv2"], J * PV2 + pvi + 1)
                        act.wait_ge(s["ovt"], 1 + J * 2 + c)
                        act.activation(OV[:, :], PV[:, :], ACT.Copy).then_inc(s["ov"], 1)
                    if not last:
                        q_with_max(j + 1)

                q_turned(b * HPG)
                q_with_max(0)
                with act.Fori(0, HPG - 1) as j:
                    heads_of(j, False)
                heads_of(HPG - 1, True)
                act.wait_ge(s["aoT"], b + 1)
                act.activation(HT[:, :], SC[:, 0, :], ACT.Copy).then_inc(s["aoTc"], 1)
                inverse_root(3)
                act.wait_ge(s["h4T"], 1 + b + 1)
                act.activation(HT[:, :], SC[:, 0, :], ACT.Copy).then_inc(s["h4Tc"], 1)
                act.wait_ge(s["lg"], b * 2 + 2)
                act.activation(W8[:, :, :], L8[:, :, :], ACT.Exp).then_inc(s["rt"], 1)
                with act.Fori(0, E // 2) as ee:
                    for k in range(2):
                        for t in range(4):
                            act.wait_ge(s["up"], (b * E + ee * 2 + k) * 4 + t + 1)
                            act.activation(SG[:, t % 2, :], SC[:, t % 2, 0:CH], ACT.Silu).then_inc(s["silu"], 1)

        @block.vector
        def _(dve):
            link0 = Chain(dve, s["one"])
            link = link0.link
            dve.memset(KL[:, :].bitcast(F32), 0.0).then_inc(s["const"], 1)
            dve.memset(V1[:, :, :], 1.0).then_inc(s["const"], 1)
            dve.memset(Q2[0][:, :].bitcast(F32), 0.0).then_inc(s["const"], 1)
            dve.memset(Q2[1][:, :].bitcast(F32), 0.0).then_inc(s["const"], 1)
            dve.memset(KT[:, :, :].bitcast(F32), 0.0).then_inc(s["const"], 1)
            dve.memset(QSJ[:, :, :, :].bitcast(F32), 0.0).then_inc(s["const"], 1)
            dve.memset(V2[:, :, :, :], 0.0).then_inc(s["const"], 1)
            dve.memset(M2[:, :, :, :], LOW).then_inc(s["const"], 1)
            dve.wait_ge(s["const"], 8)
            dve.memset(KL[64:65, :].bitcast(F32), 1.0).then_inc(s["const"], 1)
            dve.memset(V2[:, :, :, HD:2 * HD], 1.0).then_inc(s["const"], 1)
            dve.wait_ge(s["csil"], 1)
            for b in range(B):
                last = dve.tensor_copy(cbc[:, b, :], csil[:, b:b + 1].to_broadcast([128, 128]))
            last.then_inc(s["cbc"], 1)
            dve.wait_ge(s["mod"], 1)
            for b in range(B):
                last = dve.tensor_copy(mods[:, b, 0:3, :], MX[:, 0:384].rearrange("p (k d) -> p k d", k=3)) if b == 0 else \
                    dve.tensor_copy(mods[:, b, 0:3, :], PV[:, 0:384].rearrange("p (k d) -> p k d", k=3))
                last = dve.tensor_copy(mods[:, b, 3:6, :], MX[:, 512:896].rearrange("p (k d) -> p k d", k=3)) if b == 0 else \
                    dve.tensor_copy(mods[:, b, 3:6, :], XP[:, 0:384].rearrange("p (k d) -> p k d", k=3))
            link(last)
            for b in range(B):
                for k in (1, 4):
                    link(dve.tensor_scalar(mods[:, b, k, :], mods[:, b, k, :], 1.0, None, ALU.add))
                for k in (2, 5):
                    link(dve.tensor_scalar(gsgn[:, :], mods[:, b, k, :], 0.0, 2.0, ALU.is_ge, ALU.mult))
                    link(dve.scalar_tensor_tensor(out=mods[:, b, k, :], in0=gsgn[:, :], scalar=1.0,
                                                  in1=mods[:, b, k, :], op0=ALU.subtract, op1=ALU.mult))
                    link(dve.tensor_scalar(mods[:, b, k, :], mods[:, b, k, :], 0.25, None, ALU.max))
                    link(dve.scalar_tensor_tensor(out=mods[:, b, k, :], in0=gsgn[:, :], scalar=1.0,
                                                  in1=mods[:, b, k, :], op0=ALU.subtract, op1=ALU.mult))
            dve.wait_ge(s["small"], 16 * 15)
            dve.wait_ge(s["io"], 1)
            dve.wait_ge(s["tri"], 1)
            with dve.Fori(0, B) as b:
                ch = Chain(dve, s["dve"])
                ch.base = b * DVE_STEPS
                link = ch.link

                def tt(o, x, y, op):
                    return dve.tensor_tensor(o, x, y, op)

                def inverse_root(k):
                    dve.wait_ge(s["r0"], b * 8 + 2 * k + 2)
                    link(tt(st[:, 5, :], st[:, 4, :], st[:, 4, :], ALU.mult))
                    link(tt(st[:, 5, :], st[:, 5, :], st[:, 2, :], ALU.mult))
                    link(dve.tensor_scalar(st[:, 5, :], st[:, 5, :], -0.5, 1.5, ALU.mult, ALU.add))
                    link(tt(st[:, 5, :], st[:, 5, :], st[:, 4, :], ALU.mult))

                def mean_square(x, k):
                    link(tt(TB[:, :, :], x, x, ALU.mult))
                    link(dve.tensor_reduce(st[:, 1, :], TB[:, :, :], AX_X, ALU.add))
                    dve.tensor_scalar(st[:, 2, :], st[:, 1, :], 1.0 / D, EPS, ALU.mult, ALU.add).then_inc(s["var"], 1)

                def layer_norm(x, o, k, shift, scale):
                    link(dve.tensor_reduce(st[:, 0, :], x, AX_X, ALU.add))
                    link(dve.tensor_scalar(st[:, 0, :], st[:, 0, :], -1.0 / D, None, ALU.mult))
                    link(tt(o, x, per_token(st[:, 0, :]), ALU.add))
                    mean_square(o, k)
                    inverse_root(k)
                    link(tt(o, o, per_token(st[:, 5, :]), ALU.mult))
                    link(tt(o, o, bc(scale), ALU.mult))
                    return tt(o, o, bc(shift), ALU.add)

                def rms_norm(x, o, k, weight):
                    mean_square(x, k)
                    inverse_root(k)
                    link(tt(o, x, per_token(st[:, 5, :]), ALU.mult))
                    return tt(o, o, bc(weight), ALU.mult)

                dve.wait_ge(s["xld"], b * 16 + 16)
                dve.wait_ge(s["h4T"], 1 + b)
                layer_norm(X[:, :, :], HA[:, :, :], 0, mods[:, b, 0, :], mods[:, b, 1, :]).then_inc(s["h"], 1)
                dve.wait_ge(s["kv"], b + 1)
                link(dve.tensor_scalar(KK[:, :], SC[:, 1, :], bks[:, 0:1], None, ALU.add))
                dve.scalar_tensor_tensor(out=KL[0:64, :], in0=SC[0:64, 1, :], scalar=bks[0:64, 0:1],
                                         in1=KK[0:64, :].bitcast(F32), op0=ALU.add, op1=ALU.subtract)
                tt(V1[:, :, 0:DK], MX[:, 0:CH].rearrange("p (t d) -> p t d", d=DK), bc(bvs[:, :]), ALU.add).then_inc(s["kvx"], 1)

                def split(p, u, first=False):
                    unit = b * (PAIRS * UNITS) + p * UNITS + u
                    dve.wait_ge(s["qf"], b * (2 * PAIRS) + p * 2 + u // 2 + 1)
                    if not first:
                        dve.wait_ge(s["main"], 1 + (unit - 1) * STEPS)
                    src = QF[0:64, :] if u % 2 == 0 else QF[64:128, :]
                    hi = QS[0][0:64, :] if u % 2 == 0 else QS[1][64:128, :]
                    lo = QS[0][64:128, :] if u % 2 == 0 else QS[1][0:64, :]
                    link(dve.tensor_copy(hi, src))
                    dve.tensor_copy(Q2[u % 2][0:64, :], src)
                    tt(lo, src, hi.bitcast(F32), ALU.subtract).then_inc(s["qs"], 1)

                def max_of(p, u, t):
                    unit = b * (PAIRS * UNITS) + p * UNITS + u
                    dve.wait_ge(s["mx"], unit * STEPS + t + 1)
                    if t == 0:
                        dve.wait_ge(s["mt"], 1 + unit)
                    dve.tensor_reduce(MC[:, t:t + 1], MX[:, :], AX_X, ALU.max, negate=True).then_inc(s["mred"], 1)

                def max_out(p, u):
                    unit = b * (PAIRS * UNITS) + p * UNITS + u
                    dve.wait_ge(s["mt"], 1 + unit + 1)
                    dve.wait_ge(s["mdma"], 16 + unit * 16)
                    dve.tensor_copy(MR[:, :], XP[0:STEPS, 0:128]).then_inc(s["mrow"], 1)

                def norm(p, u, part):
                    unit = b * (PAIRS * UNITS) + p * UNITS + u
                    if part == 0:
                        dve.wait_ge(s["rd"], unit * 2 + 2)
                        link(tt(LD[64:128, :], OE[64:128, :], RD[64:128, :], ALU.mult))
                    elif part == 1:
                        link(dve.scalar_tensor_tensor(out=RD[0:64, :], in0=LD[64:128, :], scalar=2.0, in1=RD[64:128, :],
                                                      op0=ALU.subtract, op1=ALU.mult))
                    else:
                        lo = 64 * (u % 2)
                        dve.scalar_tensor_tensor(out=AT[lo:lo + 64, p, (u // 2) * CH:(u // 2) * CH + CH], in0=OE[0:64, :],
                                                 scalar=-1.0, in1=RD[0:64, :], op0=ALU.mult, op1=ALU.mult).then_inc(s["norm"], 1)

                def after(p, u, n):
                    return (p, u + n) if u + n < UNITS else (p + 1, u + n - UNITS)

                def unit_ops(p, u, first, last):
                    before = (p, u - 1) if u else (p - 1, UNITS - 1)
                    any_before = not (first and u == 0)
                    one, two = not (last and u == 3), not (last and u >= 2)
                    if one:
                        max_of(*after(p, u, 1), 1)
                        max_of(*after(p, u, 1), 2)
                    if any_before:
                        norm(*before, 0)
                    if one:
                        max_of(*after(p, u, 1), 3)
                    if any_before:
                        norm(*before, 1)
                    if one:
                        max_out(*after(p, u, 1))
                    if any_before:
                        norm(*before, 2)
                    if two:
                        split(*after(p, u, 2))
                        max_of(*after(p, u, 2), 0)

                dve.wait_ge(s["op"], 1 + b)
                split(0, 0, first=True)
                split(0, 1, first=True)
                for t in range(STEPS):
                    max_of(0, 0, t)
                max_out(0, 0)
                max_of(0, 1, 0)
                for u in range(UNITS):
                    unit_ops(0, u, True, False)
                n0 = ch.n
                with dve.Fori(1, PAIRS - 1) as p:
                    ch.base = b * DVE_STEPS + (p - 1) * DVE_PAIR
                    for u in range(UNITS):
                        unit_ops(p, u, False, False)
                    got = ch.n - n0
                assert got == DVE_PAIR, got
                ch.base = b * DVE_STEPS
                ch.n = n0 + (PAIRS - 2) * DVE_PAIR
                for u in range(UNITS):
                    unit_ops(PAIRS - 1, u, False, True)
                for part in range(3):
                    norm(PAIRS - 1, UNITS - 1, part)

                dve.wait_ge(s["opT"], b + 1)
                link(tt(X1[:, :, :], tiles(SC[:, 1, :]), bc(mods[:, b, 2, :]), ALU.mult))
                link(tt(X1[:, :, :], X1[:, :, :], X[:, :, :], ALU.add))
                dve.sem_inc(s["x1"], 1)
                link(layer_norm(X1[:, :, :], H2[:, :, :], 1, mods[:, b, 3, :], mods[:, b, 4, :]))
                rms_norm(H2[:, :, :], HA[:, :, :], 2, lns[:, 0, :]).then_inc(s["h3"], 1)

                dve.wait_ge(s["qkvc"], b + 1)
                nqk = QKV - NG * HD
                half = HD // 2
                for t in range(NT):
                    q3 = qkv[:, t, 0:nqk].rearrange("p (h d) -> p h d", d=HD)
                    r3 = qkr[:, t, :].rearrange("p (h d) -> p h d", d=HD)
                    tt(r3[:, :, 0:half], q3[:, :, half:HD], ropes[:, t, 1, 0:half].unsqueeze(1).to_broadcast([128, nqk // HD, half]), ALU.mult)
                    tt(r3[:, :, half:HD], q3[:, :, 0:half], ropes[:, t, 1, half:HD].unsqueeze(1).to_broadcast([128, nqk // HD, half]), ALU.mult)
                    last = tt(qko[:, t, :].rearrange("p (h d) -> p h d", d=HD), q3, ropes[:, t, 0, :].unsqueeze(1).to_broadcast([128, nqk // HD, HD]), ALU.mult)
                link(last)
                link(tt(qkr[:, :, :], qkr[:, :, :], qko[:, :, :], ALU.add))
                dve.tensor_copy(V2[:, :, :, 0:HD], qkv[:, :, nqk:QKV].rearrange("p t (g d) -> p t g d", g=NG)).then_inc(s["vset"], 1)
                k4 = qkr[:, :, 128:nqk].rearrange("p t (g d) -> p t g d", g=NG)
                link(dve.tensor_copy(KS[:, :, :, 0:8], k4))
                dve.tensor_copy(KS[:, :, :, 8:16], k4)
                tt(KS[:, :, :, 16:24], k4, KS[:, :, :, 0:8].bitcast(F32), ALU.subtract)
                dve.memset(KS[:, :, :, MROW:MROW + 1].bitcast(F32), 1.0).then_inc(s["ks"], 1)
                dve.wait_ge(s["kT"], b + 1)
                plain(dve)

                def stack_q(j):
                    J = b * HPG + j
                    q4 = qkr[:, :, 0:128].rearrange("p t (g j d) -> p j t g d", g=NG, j=HPG)[:, j]
                    dve.wait_ge(s["tb"], 1 + J)
                    plain(dve)
                    link(dve.tensor_copy(QSJ[:, :, :, 0:8], q4))
                    plain(dve)
                    dve.tensor_copy(QSJ[:, :, :, 16:24], q4)
                    dve.memset(QSJ[:, :, :, MROW:MROW + 1].bitcast(F32), 0.0)
                    tt(QSJ[:, :, :, 8:16], q4, QSJ[:, :, :, 0:8].bitcast(F32), ALU.subtract).then_inc(s["qsj"], 1)

                def reduce_pieces(J, step):
                    for t, g, piece, k0, w in pieces(step):
                        i = item(t, g, piece)
                        dve.wait_ge(s["m2"], J * ITEMS + i + 1)
                        if i >= 4:
                            dve.wait_ge(s["m2red"], J * ITEMS + i - 2)
                        plain(dve)
                        src = MX[:, (i % 2) * CH:(i % 2) * CH + w]
                        if piece:
                            ins = dve.tensor_tensor_reduce(out=junk[:, i % 4, 0:w], in0=src, in1=tri[:, CH - w:CH], scale=1.0,
                                                           scalar=-3.0e38, op0=ALU.add, op1=ALU.max, accum_out=M2[:, t, g, 0:1])
                        else:
                            ins = dve.tensor_reduce(M2[:, t, g, 1:2], src, AX_X, ALU.max)
                        ins.then_inc(s["m2red"], 1)

                def stack_max(J):
                    dve.wait_ge(s["m2red"], 1 + J * ITEMS + ITEMS)
                    dve.tensor_reduce(QSJ[:, :, :, MROW:MROW + 1], M2[:, :, :, :], AX_X, ALU.max, negate=True).then_inc(s["qsm"], 1)

                def divide(j, c):
                    J = b * HPG + j
                    dve.wait_ge(s["ovt"], 1 + J * 2 + c + 1)
                    x4 = XP[:, :].rearrange("p (t g r) -> p t g r", t=4, g=NG)
                    link(dve.reciprocal(RC[:, :, :], x4[:, :, :, HD]))
                    link(tt(AO[:, 4 * c:4 * c + 4, :].rearrange("p t (g j d) -> p j t g d", g=NG, j=HPG)[:, j],
                            x4[:, :, :, 0:HD], RC[:, :, :].unsqueeze(3).to_broadcast([128, 4, NG, HD]), ALU.mult))
                    dve.sem_inc(s["ao"], 1)

                def heads_of(j, last):
                    if not last:
                        stack_q(j + 1)
                    for step in range(PV2):
                        if not last:
                            reduce_pieces(b * HPG + j + 1, step)
                        if step == 6:
                            divide(j, 0)
                    if not last:
                        stack_max(b * HPG + j + 1)
                    divide(j, 1)

                stack_q(0)
                reduce_pieces(b * HPG, None)
                stack_max(b * HPG)
                n0 = ch.n
                with dve.Fori(0, HPG - 1) as j:
                    ch.base = b * DVE_STEPS + j * DVE_J
                    heads_of(j, False)
                    got = ch.n - n0
                assert got == DVE_J, got
                ch.base = b * DVE_STEPS
                ch.n = n0 + (HPG - 1) * DVE_J
                heads_of(HPG - 1, True)

                dve.wait_ge(s["wo2"], b + 1)
                link(tt(H2[:, :, :], tiles(SC[:, 1, :]), H2[:, :, :], ALU.add))
                rms_norm(H2[:, :, :], HA[:, :, :], 3, lns[:, 1, :]).then_inc(s["h4"], 1)
                dve.wait_ge(s["lg"], b * 2 + 1)
                link(dve.tensor_copy(L8[:, :, :], XP[:, 0:NT * E].rearrange("p (t e) -> p t e", e=E)))
                plain(dve)
                for t in range(NT):
                    last = dve.max(T8[:, t, :], L8[:, t, :])
                link(last)
                plain(dve)
                for t in range(NT):
                    last = dve.max_index(I8[:, t, :], T8[:, t, :], L8[:, t, :])
                link(last)
                link(tt(L8[:, :, :], L8[:, :, :], T8[:, :, 0:1].to_broadcast([128, NT, E]), ALU.subtract))
                dve.sem_inc(s["lg"], 1)
                link(dve.tensor_copy(IF[:, :, :], I8[:, :, 0:2]))
                link(tt(WF[:, :, :], bc(io8[:, :]), IF[:, :, 0:1].to_broadcast([128, NT, E]), ALU.is_equal))
                link(tt(T8[:, :, :], bc(io8[:, :]), IF[:, :, 1:2].to_broadcast([128, NT, E]), ALU.is_equal))
                link(tt(WF[:, :, :], WF[:, :, :], T8[:, :, :], ALU.add))
                dve.wait_ge(s["rt"], b + 1)
                link(tt(WF[:, :, :], WF[:, :, :], W8[:, :, :], ALU.mult))
                link(dve.tensor_reduce(st[:, 6, :], WF[:, :, :], AX_X, ALU.add))
                link(dve.reciprocal(st[:, 7, :], st[:, 6, :]))
                link(tt(WF[:, :, :], WF[:, :, :], per_token(st[:, 7, :], E), ALU.mult))
                link(dve.memset(ACC[:, :, :], 0.0))
                dve.wait_ge(s["out"], 16 + b * 16)
                plain(dve)
                with dve.Fori(0, E // 2) as ee:
                    for k in range(2):
                        n = b * E + ee * 2 + k

                        def gated(t):
                            dve.wait_ge(s["silu"], n * 4 + t + 1)
                            tt(G[:, t // 2, t % 2, :], SG[:, t % 2, :], SC[:, t % 2, CH:2 * CH], ALU.mult).then_inc(s["g"], 1)

                        def accumulate(c):
                            if c == 0:
                                dve.wait_ge(s["down"], n + 1)
                            else:
                                dve.wait_ge(s["slot"], n + 3)
                            tt(TA[:, 4 * c:4 * c + 4, :], tiles(MX[:, c * CH:(c + 1) * CH]),
                               WF[:, 4 * c:4 * c + 4, bass.ds(ee * 2 + k, 1)].to_broadcast([128, 4, D]), ALU.mult).then_inc(s["accfree"], 1)
                            dve.wait_ge(s["accfree"], n * 2 + c + 3)
                            tt(ACC[:, 4 * c:4 * c + 4, :], ACC[:, 4 * c:4 * c + 4, :], TA[:, 4 * c:4 * c + 4, :], ALU.add).then_inc(s["mods"], 1)

                        gated(0)
                        gated(1)
                        gated(2)
                        gated(3)
                        dve.wait_ge(s["mods"], 1 + n * 2)
                        accumulate(0)
                        accumulate(1)
                dve.wait_ge(s["mods"], 1 + b * (2 * E) + 2 * E)
                link(tt(TA[:, :, :], ACC[:, :, :], H2[:, :, :], ALU.add))
                link(tt(TA[:, :, :], TA[:, :, :], bc(mods[:, b, 5, :]), ALU.mult))
                tt(TA[:, :, :], TA[:, :, :], X1[:, :, :], ALU.add).then_inc(s["y"], 1)
                assert ch.n == DVE_STEPS, ch.n

        @block.tensor
        def _(pe):
            mm = pe.matmul
            pe.wait_ge(s["idn"], 3)
            pe.wait_ge(s["wmodld"], 32)
            pe.wait_ge(s["const"], 10)
            pe.wait_ge(s["cbc"], 1)
            for o, b, c in ((MX[:, 0:384], 0, 0), (MX[:, 512:896], 0, 1), (PV[:, 0:384], 1, 0), (XP[:, 0:384], 1, 1)):
                last = mm(o, cbc[:, b, :], wmods[:, c * 384:(c + 1) * 384], start=True, stop=True)
            last.then_inc(s["mod"], 1)
            pe.wait_ge(s["small"], 16 * 15)
            pe.wait_ge(s["one"], 21)
            with pe.Fori(0, B) as b:
                def transposes(src, half):
                    for t in range(NT):
                        last = pe.transpose(SC[:, half, t * 128:t * 128 + 128], src[:, t, :], ident[:, :])
                    return last

                pe.wait_ge(s["h"], b + 1)
                transposes(HA, 0).then_inc(s["hT"], 1)
                pe.wait_ge(s["hTc"], b + 1)
                for c in range(NC):
                    mm(SC[:, 1, c * CH:(c + 1) * CH], wk2[:, :], HT[:, c * CH:(c + 1) * CH], start=True, stop=True)
                for t in range(NT):
                    last = mm(MX[:, t * DK:(t + 1) * DK], HT[:, t * 128:(t + 1) * 128], wvs[:, :], start=True, stop=True)
                last.then_inc(s["kv"], 1)

                def q_proj(p, c, first=False):
                    pe.wait_ge(s["wqld"], (b * PAIRS + p) * 16 + 16)
                    pe.wait_ge(s["mrow"], (b * (2 * PAIRS) + p * 2 + c) * 2 + (1 if first else 0))
                    mm(XP[:, :], wqs[:, :], HT[:, c * CH:(c + 1) * CH], start=True, stop=True).then_inc(s["q"], 1)

                def max_pass(p, u, t):
                    unit = b * (PAIRS * UNITS) + p * UNITS + u
                    if t == 0:
                        pe.wait_ge(s["qs"], 1 + unit + 1)
                    pe.wait_ge(s["mred"], 1 + unit * STEPS + t)
                    q = QS[u % 2][:, t * 128:(t + 1) * 128]
                    mm(MX[:, 0:CH], q, KK[:, 0:CH], start=True, stop=True)
                    mm(MX[:, CH:S], q, KK[:, CH:S], start=True, stop=True).then_inc(s["mx"], 1)

                def max_turn(p, u, last=False):
                    unit = b * (PAIRS * UNITS) + p * UNITS + u
                    begun = u // 2 + 1 + (1 if u % 2 and not last else 0)
                    pe.wait_ge(s["mred"], 1 + unit * STEPS + STEPS)
                    pe.wait_ge(s["qf"], b * (2 * PAIRS) + p * 2 + begun)
                    pe.wait_ge(s["mrow"], 1 + unit)
                    pe.transpose(XP[0:STEPS, 0:128], MC[:, :], ident[:, :]).then_inc(s["mt"], 1)

                def scores(unit, u, t):
                    if t >= 2:
                        pe.wait_ge(s["exp"], unit * STEPS + t - 1)
                    for k in range(2):
                        kt = 2 * t + k
                        mm(SC[:, t % 2, k * CH:(k + 1) * CH], KK[:, kt * 128:(kt + 1) * 128], QS[u % 2][:, :], start=True, stop=False)
                    if t == 0:
                        pe.wait_ge(s["mdma"], 16 + unit * 16 + 16)
                    for k in range(2):
                        kt = 2 * t + k
                        last = mm(SC[:, t % 2, k * CH:(k + 1) * CH], KL[:, kt * 128:(kt + 1) * 128], Q2[u % 2][:, :], start=False, stop=True)
                    last.then_inc(s["main"], 1)

                def weigh(unit, t, half):
                    if half == 0:
                        pe.wait_ge(s["exp"], unit * STEPS + t + 1)
                        if t == 0:
                            pe.wait_ge(s["pve"], 1 + unit)
                    kt = 2 * t + half
                    last = mm(PV[:, :], V1[:, kt, :], P[:, t % 2, half, :], start=(kt == 0), stop=(kt == NT - 1))
                    if half == 1:
                        last.then_inc(s["pv"], 1)

                def after(p, u, n):
                    return (p, u + n) if u + n < UNITS else (p + 1, u + n - UNITS)

                def unit_mms(p, u, last):
                    unit = b * (PAIRS * UNITS) + p * UNITS + u
                    one, two = not (last and u == 3), not (last and u >= 2)
                    if one:
                        max_pass(*after(p, u, 1), 1)
                    scores(unit, u, 1)
                    weigh(unit, 0, 0)
                    if two and u % 2 == 0:
                        nq = after(p, u, 2)
                        q_proj(nq[0], nq[1] // 2)
                    if one:
                        max_pass(*after(p, u, 1), 2)
                    weigh(unit, 0, 1)
                    scores(unit, u, 2)
                    if one:
                        max_pass(*after(p, u, 1), 3)
                    weigh(unit, 1, 0)
                    weigh(unit, 1, 1)
                    if one:
                        max_turn(*after(p, u, 1), last and u == 2)
                    scores(unit, u, 3)
                    weigh(unit, 2, 0)
                    weigh(unit, 2, 1)
                    if one:
                        scores(unit + 1, (u + 1) % UNITS, 0)
                    if two:
                        max_pass(*after(p, u, 2), 0)
                    weigh(unit, 3, 0)
                    weigh(unit, 3, 1)

                q_proj(0, 0, first=True)
                pe.wait_ge(s["kvx"], b + 1)
                for t in range(STEPS):
                    max_pass(0, 0, t)
                max_turn(0, 0)
                scores(b * (PAIRS * UNITS), 0, 0)
                max_pass(0, 1, 0)
                with pe.Fori(0, PAIRS - 1) as p:
                    for u in range(UNITS):
                        unit_mms(p, u, False)
                for u in range(UNITS):
                    unit_mms(PAIRS - 1, u, True)
                pe.wait_ge(s["norm"], 1 + b * (PAIRS * UNITS) + PAIRS * UNITS)
                for c in range(NC):
                    for p in range(PAIRS):
                        last = mm(SC[:, 0, c * CH:(c + 1) * CH], wos[:, p, :], AT[:, p, c * CH:(c + 1) * CH],
                                  start=(p == 0), stop=(p == PAIRS - 1))
                last.then_inc(s["op"], 1)
                pe.wait_ge(s["opc"], b + 1)
                transposes(TA, 1).then_inc(s["opT"], 1)
                pe.wait_ge(s["h3"], b + 1)
                transposes(HA, 0).then_inc(s["h3T"], 1)
                pe.wait_ge(s["h3Tc"], b + 1)
                for t in range(NT):
                    last = mm(SCF[:, t * 256:t * 256 + QKV], HT[:, t * 128:(t + 1) * 128], WQKVT[:, 0:QKV], start=True, stop=True)
                last.then_inc(s["qkv"], 1)
                pe.wait_ge(s["ks"], b + 1)
                pe.wait_ge(s["qkvc"], b + 1)

                def turn_stack(o):
                    for t in range(NT):
                        last = pe.transpose(o[:, t * 128:t * 128 + 128], QSJ[:, t, :, :].rearrange("p g r -> p (g r)").bitcast(F32), ident[:, :])
                    return last

                turn_stack(SC[:, 0, :]).then_inc(s["kT"], 1)
                pe.wait_ge(s["kTc"], b + 1)
                pe.wait_ge(s["vset"], b + 1)

                def max_pieces(J, step):
                    for t, g, piece, k0, w in pieces(step):
                        i = item(t, g, piece)
                        if i == 0:
                            pe.wait_ge(s["qta"], J + 1)
                        pe.wait_ge(s["m2red"], 1 + J * ITEMS + max(0, i - 1))
                        mm(MX[:, (i % 2) * CH:(i % 2) * CH + w], QTA[:, t * 128:(t + 1) * 128], KT[:, g, k0:k0 + w],
                           start=True, stop=True).then_inc(s["m2"], 1)

                def turn_q(J):
                    pe.wait_ge(s["qsj"], J + 1)
                    turn_stack(MX).then_inc(s["ta"], 1)

                def turn_q_with_max(J):
                    pe.wait_ge(s["qsm"], J + 1)
                    turn_stack(MX).then_inc(s["tb"], 1)

                def heads_of(j, last):
                    J = b * HPG + j
                    pe.wait_ge(s["qtb"], J + 1)
                    if last:
                        plain(pe)

                    def weigh2(c, kt):
                        off, cnt = rows((c, kt))
                        pvi = 4 * c + kt
                        pe.wait_ge(s["exp2"], J * ST2 + (8 if c else 0) + 2 * kt + 2)
                        if kt >= 4 * c:
                            pe.wait_ge(s["tri2"], J * 16 + 8 * c + 2 * (kt - 4 * c) + 2)
                        if kt == 0:
                            pe.wait_ge(s["ov"], 1 + J * 2 + c)
                        for g in range(NG):
                            last = mm(PV[32 * g:32 * g + 32, off:CH], V2[:, kt, g, :], P[:, pvi % 2, g, off:CH],
                                      start=(kt == 0), stop=(kt == 4 * c + 3))
                        last.then_inc(s["pv2"], 1)

                    def turn_out(c):
                        pe.wait_ge(s["ov"], 1 + J * 2 + c + 1)
                        pe.wait_ge(s["ao"], 1 + J * 2 + c)
                        for t in range(4):
                            last = pe.transpose(XP[:, t * 128:(t + 1) * 128], OV[:, t * 128:(t + 1) * 128], ident[:, :])
                        last.then_inc(s["ovt"], 1)

                    n = 0
                    for c in range(NC):
                        for kt in range(4 * c + 4):
                            off, cnt = rows((c, kt))
                            step = 4 * c + kt
                            for hh in range(2):
                                if n >= 2:
                                    pe.wait_ge(s["exp2"], J * ST2 + n - 1)
                                for g in (2 * hh, 2 * hh + 1):
                                    mn = mm(SC[:, n % 2, (g % 2) * CH + off:(g % 2) * CH + CH], KT[:, g, kt * 128:(kt + 1) * 128],
                                            QTB[:, j, c * CH + off:(c + 1) * CH], start=True, stop=True)
                                mn.then_inc(s["main2"], 1)
                                n += 1
                            if step == 1 and not last:
                                turn_q(J + 1)
                            if kt > 0:
                                weigh2(c, kt - 1)
                            elif c == 1:
                                weigh2(0, 3)
                            if not last:
                                max_pieces(J + 1, step)
                            if step == 6:
                                turn_out(0)
                    weigh2(1, 7)
                    if not last:
                        turn_q_with_max(J + 1)
                    turn_out(1)

                turn_q(b * HPG)
                max_pieces(b * HPG, None)
                turn_q_with_max(b * HPG)
                with pe.Fori(0, HPG - 1) as j:
                    heads_of(j, False)
                heads_of(HPG - 1, True)
                pe.wait_ge(s["ao"], 1 + b * (2 * HPG) + 2 * HPG)
                transposes(AO, 0).then_inc(s["aoT"], 1)
                pe.wait_ge(s["aoTc"], b + 1)
                for t in range(NT):
                    last = mm(SC[:, 1, t * 128:(t + 1) * 128], HT[:, t * 128:(t + 1) * 128], WOT[:, :], start=True, stop=True)
                last.then_inc(s["wo2"], 1)
                pe.wait_ge(s["h4"], b + 1)
                transposes(HA, 0).then_inc(s["h4T"], 1)
                pe.wait_ge(s["h4Tc"], b + 1)
                for t in range(NT):
                    last = mm(XP[:, t * E:(t + 1) * E], HT[:, t * 128:(t + 1) * 128], gates[:, :], start=True, stop=True)
                last.then_inc(s["lg"], 1)
                with pe.Fori(0, E // 2) as ee:
                    for k in range(2):
                        n = b * E + ee * 2 + k

                        def up(t):
                            if t == 0:
                                pe.wait_ge(s["wcopy"], n + 1)
                            if t >= 2:
                                pe.wait_ge(s["g"], n * 4 + t - 1)
                            c, f = t // 2, t % 2
                            mm(SC[:, t % 2, 0:CH], W13S[k][:, f * 128:(f + 1) * 128], HT[:, c * CH:(c + 1) * CH], start=True, stop=True)
                            mm(SC[:, t % 2, CH:2 * CH], W13S[k][:, FFN + f * 128:FFN + (f + 1) * 128], HT[:, c * CH:(c + 1) * CH],
                               start=True, stop=True).then_inc(s["up"], 1)

                        def down(c):
                            pe.wait_ge(s["g"], n * 4 + 2 * c + 2)
                            pe.wait_ge(s["accfree"], n * 2 + c + 1)
                            for t in range(4):
                                for f in range(2):
                                    last = mm(MX[:, c * CH + t * 128:c * CH + (t + 1) * 128], G[:, c, f, t * 128:(t + 1) * 128],
                                              W2S[k][:, f * D:(f + 1) * D], start=(f == 0), stop=(f == 1))
                            last.then_inc(s["down"] if c == 0 else s["slot"], 1)

                        up(0)
                        up(1)
                        up(2)
                        down(0)
                        up(3)
                        down(1)


_INS = ["L0_attn_x", "L0_attn_Wq", "L0_attn_bq", "L0_attn_Wk", "L0_attn_bk", "L0_attn_Wv", "L0_attn_bv", "L0_attn_Wo",
        "L0_attn_bo", "L0_ffn_ln1_w", "L0_ffn_ln2_w", "L0_ffn_wqkv", "L0_ffn_wo", "L0_ffn_gate_w", "L0_ffn_w13",
        "L0_ffn_w2", "L0_c", "L0_wmod"]


def kernel(**inputs):
    import numpy as np
    import concourse.bacc as bacc
    from concourse.bass_utils import run_bass_kernel_spmd

    nc = bacc.Bacc("TRN2", target_bir_lowering=False, num_devices=1)
    lay = {
        "L0_attn_bq": lambda a: a.reshape(PAIRS, 128).T,
        "L0_ffn_wqkv": lambda a: a.T,
        "L0_ffn_wo": lambda a: a.T,
        "L0_ffn_gate_w": lambda a: a.T,
        "L0_ffn_w13": lambda a: a.transpose(2, 0, 1),
        "L0_ffn_w2": lambda a: a.reshape(E, D, 2, 128).transpose(3, 0, 2, 1).reshape(128, E, 2 * D),
        "L0_c": lambda a: a.T,
    }
    arrays, args = {}, []
    for name in _INS:
        a = np.asarray(inputs[name])
        a = np.ascontiguousarray(lay[name](a) if name in lay else a)
        arrays["in_" + name] = a
        args.append(nc.dram_tensor("in_" + name, a.shape, mybir.dt.from_np(a.dtype), kind="ExternalInput").ap())
    inv = (np.float32(1.0) / np.float32(10000.0) ** (np.arange(0, HD, 2, dtype=np.float32) / np.float32(HD))).astype(np.float32)
    ang = np.arange(S, dtype=np.float32)[:, None] * inv[None, :]
    cos, sin = np.cos(ang), np.sin(ang)
    rope = np.stack([np.concatenate([cos, cos], 1), np.concatenate([-sin, sin], 1)], 1).astype(np.float32)
    arrays["rope"] = rope
    args.append(nc.dram_tensor("rope", rope.shape, F32, kind="ExternalInput").ap())
    out = nc.dram_tensor("out_0", (B, S, D), F32, kind="ExternalOutput").ap()
    build(nc, *args, out)
    r = run_bass_kernel_spmd(nc, [arrays], core_ids=[0])
    return r.results[0]["out_0"]
```

```python
from contextlib import ExitStack

import concourse.bass as bass
from concourse import mybir

F32 = mybir.dt.float32
F32R = mybir.dt.float32r
ALU = mybir.AluOpType
ACT = mybir.ActivationFunctionType
AX_X = mybir.AxisListType.X

B, S, D = 2, 1024, 128
NT = S // 128
NC = 2
CH = S // NC
H, DK = 16, 64
PAIRS = H // 2
DUOS = PAIRS * NC
STEPS = NT
ADDS = NT - 1
MAXES = 2 * CH // 128
NG, HPG, HD = 4, 4, 8
NH2 = NG * HPG
QKV = (NH2 + 2 * NG) * HD
ROWS = 32
MROW = 24
ITEMS = 48
ST2 = 24
PV2 = 12
E, FFN = 8, 256
EPS = 1e-5
LOW = -1.0e30
DVE_STEPS = 127
DVE_PAIR = 6
DVE_J = 5


class Chain:

    def __init__(self, eng, sem):
        self.eng, self.sem, self.n, self.base = eng, sem, 0, 0

    def link(self, ins):
        self.n += 1
        ins.then_inc(self.sem, 1)
        self.eng.wait_ge(self.sem, self.base + self.n)


def rows(n):
    c, kt = n
    off = max(0, kt * 128 - c * CH)
    return off, CH - off


def item(t, g, piece):
    return 4 * t + g if t < 4 else 16 + 8 * (t - 4) + 2 * g + piece


def pieces(step):
    every = []
    for t in range(NT):
        for g in range(NG):
            if t >= 4:
                every.append((t, g, 0, 0, CH))
            every.append((t, g, 1, CH * (t // 4), (t % 4 + 1) * 128))
    return every if step is None else every[5 * (step - 2):5 * (step - 1)] if step >= 2 else []


def build(nc, a_x, Wq, bq, Wk, bk, Wv, bv, Wo, bo, ln1, ln2, wqkv, wo, gate, w13, w2, cin, wmod, rope, out):
    with ExitStack() as ctx:
        def sb(name, shape, dt=F32):
            return ctx.enter_context(nc.sbuf_tensor(name, shape, dt))

        def ps(name, shape):
            return ctx.enter_context(nc.psum_tensor(name, shape, F32))

        def sem(name):
            return ctx.enter_context(nc.semaphore(name))

        SC = ps("SC", [128, 2, 1024])
        SCF = SC[:, :, :].rearrange("p a b -> p (a b)")
        MX = ps("MX", [128, 1024])
        PV = ps("PV", [128, CH])
        XP = ps("XP", [128, CH])

        ident = sb("ident", [128, 128])
        tri = sb("tri", [128, CH])
        wk2 = sb("wk2", [128, 128])
        wvs = sb("wvs", [128, DK])
        wos = sb("wos", [128, PAIRS, D])
        bqs = sb("bqs", [128, PAIRS])
        bks = sb("bks", [128, 1])
        bvs = sb("bvs", [128, DK])
        bos = sb("bos", [128, 1])
        lns = sb("lns", [128, 2, D])
        cs = sb("cs", [128, B])
        csil = sb("csil", [128, B])
        cbc = sb("cbc", [128, B, 128])
        wmods = sb("wmods", [128, 6 * D])
        mods = sb("mods", [128, B, 6, D])
        gsgn = sb("gsgn", [128, D])
        gates = sb("gates", [128, E])
        ropes = sb("ropes", [128, NT, 2, HD])
        BIG = sb("BIG", [128, PAIRS * S])
        AT = BIG[:, :].rearrange("p (j n) -> p j n", j=PAIRS)
        W13T = sb("W13T", [128, E, 2 * FFN])
        W2T = sb("W2T", [128, E, 2 * D])
        WQKVT = sb("WQKVT", [128, QKV])
        WOT = sb("WOT", [128, D])

        X = sb("X", [128, NT, D])
        X1 = sb("X1", [128, NT, D])
        HA = sb("HA", [128, NT, D])
        H2 = sb("H2", [128, NT, D])
        TA = sb("TA", [128, NT, D])
        TB = sb("TB", [128, NT, D])
        HT = sb("HT", [128, S])
        st = sb("st", [128, 8, NT])
        wqs = sb("wqs", [128, 128])
        KK = sb("KK", [128, S], F32R)
        KL = sb("KL", [128, S], F32R)
        V1 = sb("V1", [128, NT, DK])
        ones = sb("ones", [128, DK])
        QF = sb("QF", [128, CH])
        Q2 = [sb(f"Q2{i}", [128, 2 * CH], F32R) for i in range(NC)]
        MC = sb("MC", [128, MAXES])
        MR = sb("MR", [MAXES, 128], F32R)
        P = sb("P", [128, 2, NG, CH])
        OE = sb("OE", [128, CH])
        LD = sb("LD", [128, CH])
        RD = sb("RD", [128, CH])
        QSJ = sb("QSJ", [128, NT, NG, ROWS], F32R)
        KT = sb("KT", [128, NG, S], F32R)
        QTA = sb("QTA", [128, S], F32R)
        QTB = sb("QTB", [128, HPG, S], F32R)
        V2 = sb("V2", [128, NT, NG, ROWS])
        M2 = sb("M2", [128, NT, NG, 2])
        RC = sb("RC", [128, 4, NG])
        L8 = sb("L8", [128, NT, E])
        T8 = sb("T8", [128, NT, 8])
        I8 = sb("I8", [128, NT, 8], mybir.dt.uint32)
        IF = sb("IF", [128, NT, 2])
        io8 = sb("io8", [128, E])
        WF = sb("WF", [128, NT, E])
        W8 = sb("W8", [128, NT, E])
        W13S = [sb(f"W13S{i}", [128, 2 * FFN]) for i in range(2)]
        W2S = [sb(f"W2S{i}", [128, 2 * D]) for i in range(2)]
        AO = TB
        QS = [[QTB[:, 2 * c + h, 0:CH] for h in range(2)] for c in range(NC)]
        TS = [x[:, :, :].rearrange("p t d -> p (t d)") for x in (TB, TA)]
        KS = QSJ
        SG = P[:, 0, 0:2, :]
        G = P[:, 1, :, :].rearrange("p (c f) q -> p c f q", c=NC)
        ACC = BIG[:, 0:S].rearrange("p (t d) -> p t d", t=NT)
        OV = BIG[:, S:S + CH]
        junk = BIG[:, 2 * S:4 * S].rearrange("p (n q) -> p n q", n=4)
        NQK = QKV - NG * HD
        qkv = BIG[:, 4 * S:4 * S + NT * QKV].rearrange("p (t n) -> p t n", t=NT)
        qkr = BIG[:, 4 * S + NT * QKV:4 * S + NT * (QKV + NQK)].rearrange("p (t n) -> p t n", t=NT)
        qko = BIG[:, 4 * S + NT * (QKV + NQK):8 * S].rearrange("p (t n) -> p t n", t=NT)

        names = """small rawld wmodld idn tri io const one turn csil cbc mod mods xld wqld dve var r0
            h hT hTc kv kvx q qf qs q2 mx mred mt mrow mdma main exp pv pve sum den n0 rd norm op opc opT x1 h3 h3T h3Tc qkv
            qkvc ks kT kTc vset qsj ta qta m2 m2red qsm tb qtb main2 exp2 tri2 pv2 ov ovt ao aoT aoTc wo2 h4 h4T
            h4Tc lg rt slot wcopy up silu g down accfree y out""".split()
        s = {n: sem("s_" + n) for n in names}
        block = ctx.enter_context(nc.Block())

        def bc(ap, n=NT):
            return ap.unsqueeze(1).to_broadcast([128, n, ap.shape[-1]])

        def per_token(ap, n=D):
            return ap.unsqueeze(2).to_broadcast([128, ap.shape[1], n])

        def tiles(ap):
            return ap.rearrange("p (t d) -> p t d", d=128)

        def buf1(kt):
            i = kt % 4
            return P[:, i // 2, 2 * (i % 2):2 * (i % 2) + 2, :].rearrange("p h q -> p (h q)")

        def after(p, c, n):
            return p + (c + n) // NC, (c + n) % NC

        def max_place(i, alone):
            return (MX[:, :], SC[:, 0, :], SC[:, 1, :])[i % 3 if alone else 0]

        def max_bank(i, alone, w):
            k = i % 6 if alone else i % 2
            return MX[:, k * CH:k * CH + w] if k < 2 else SCF[:, (k - 2) * CH:(k - 2) * CH + w]

        def plain(eng):
            eng.sem_inc(s["turn"], 1)

        STARTED = {n: 1 for n in "x1 q h4T op mt mrow mred qs q2 pve norm tb m2red ovt ov ao mods main".split()} | {"mdma": 16, "out": 16, "sum": 4}

        @block.sync
        def _(sp):
            for n, turn in STARTED.items():
                sp.sem_inc(s[n], turn)
            sp.dma_start(cs[:, :], cin).then_inc(s["wmodld"], 16)
            sp.dma_start(wmods[:, :], wmod).then_inc(s["wmodld"], 16)
            small = [
                (wk2[:, 0:DK], Wk), (wk2[:, DK:128], Wk), (wvs[:, :], Wv),
                (wos[:, :, :], Wo.rearrange("(j p) d -> p j d", p=128)),
                (bqs[:, :], bq),
                (bks[0:64, :], bk.rearrange("(p a) -> p a", a=1)), (bks[64:128, :], bk.rearrange("(p a) -> p a", a=1)),
                (bvs[:, :], bv.partition_broadcast(128)), (bos[:, :], bo.rearrange("(p a) -> p a", a=1)),
                (lns[:, 0, :], ln1.partition_broadcast(128)), (lns[:, 1, :], ln2.partition_broadcast(128)),
                (gates[:, :], gate), (WQKVT[:, :], wqkv), (WOT[:, :], wo),
                (ropes[:, :, :, :], rope.rearrange("(t p) k d -> p t k d", p=128)),
            ]
            for dst, src in small:
                sp.dma_start(dst, src).then_inc(s["small"], 16)
            sp.dma_start(W13T[:, :, :], w13).then_inc(s["rawld"], 16)
            sp.dma_start(W2T[:, :, :], w2).then_inc(s["rawld"], 16)
            with sp.Fori(0, B) as b:
                sp.wait_ge(s["x1"], 1 + b)
                sp.dma_start(X[:, :, :], a_x[b].rearrange("(t p) d -> p t d", p=128)).then_inc(s["xld"], 16)
                sp.wait_ge(s["q"], 1 + b * DUOS)
                sp.dma_start(wqs[:, :], Wq[:, 0:128]).then_inc(s["wqld"], 16)

                def next_wq(p):
                    sp.wait_ge(s["q"], 1 + b * DUOS + p * NC)
                    sp.dma_start(wqs[:, :], Wq[:, bass.ds(p * 128, 128)]).then_inc(s["wqld"], 16)

                def max_row(p, c):
                    sp.wait_ge(s["mrow"], 1 + b * DUOS + p * NC + c + 1)
                    sp.dma_start(Q2[c][64:65, :].bitcast(F32), MR[:, :].bitcast(F32)).then_inc(s["mdma"], 16)

                next_wq(1)
                max_row(0, 0)
                with sp.Fori(0, PAIRS - 2) as p:
                    max_row(p, 1)
                    next_wq(p + 2)
                    max_row(p + 1, 0)
                max_row(PAIRS - 2, 1)
                max_row(PAIRS - 1, 0)
                max_row(PAIRS - 1, 1)
                sp.wait_ge(s["y"], b + 1)
                sp.dma_start(out[b].rearrange("(t p) d -> p t d", p=128), TA[:, :, :]).then_inc(s["out"], 16)
            sp.wait_ge(s["out"], 16 + 16 * B)

        @block.gpsimd
        def _(pool):
            pool.memset(ident[:, :], 0.0).then_inc(s["idn"], 1)
            pool.memset(tri[:, :], 0.0).then_inc(s["idn"], 1)
            pool.wait_ge(s["idn"], 2)
            pool.affine_select(out=ident[:, :], in_=ident[:, :], compare_op=ALU.not_equal, fill=1.0, base=0,
                               pattern=[[-1, 128]], channel_multiplier=1).then_inc(s["idn"], 1)
            pool.affine_select(out=tri[:, CH - 128:CH], in_=tri[:, CH - 128:CH], compare_op=ALU.is_ge, fill=LOW,
                               base=0, pattern=[[-1, 128]], channel_multiplier=1).then_inc(s["tri"], 1)
            pool.iota(io8[:, :], pattern=[[1, E]], base=0, channel_multiplier=0,
                      allow_small_or_imprecise_dtypes=True).then_inc(s["io"], 1)
            pool.memset(W13S[0][:, 0:1], 0.0).then_inc(s["slot"], 2)
            pool.memset(W13S[1][:, 0:1], 0.0).then_inc(s["accfree"], 2)
            pool.wait_ge(s["slot"], 2)
            pool.wait_ge(s["accfree"], 2)
            pool.wait_ge(s["rawld"], 32)
            with pool.Fori(0, B) as b:
                pool.wait_ge(s["out"], 16 + 16 * b)
                plain(pool)
                with pool.Fori(0, PAIRS) as p:
                    for c in range(NC):
                        D = b * DUOS + p * NC + c
                        for kt in range(1, NT):
                            pool.wait_ge(s["exp"], D * STEPS + kt + 1)
                            if kt > 1:
                                pool.wait_ge(s["sum"], 4 + D * ADDS + kt - 1)
                            pool.tensor_tensor(TS[c], buf1(0) if kt == 1 else TS[c], buf1(kt), ALU.add).then_inc(s["sum"], 1)
                with pool.Fori(0, HPG) as j:
                    n = 0
                    for c in range(NC):
                        for kt in range(4 * c, 4 * c + 4):
                            stp = (8 if c else 0) + 2 * kt
                            off, _ = rows((c, kt))
                            for hh in range(2):
                                pool.wait_ge(s["exp2"], (b * HPG + j) * ST2 + stp + hh + 1)
                                plain(pool)
                                blk = P[:, (4 * c + kt) % 2, 2 * hh:2 * hh + 2, off:off + 128]
                                pool.affine_select(out=blk, in_=blk, compare_op=ALU.is_ge, fill=0.0, base=0,
                                                   pattern=[[0, 2], [1, 128]], channel_multiplier=-1).then_inc(s["tri2"], 1)
                                n += 1
                with pool.Fori(0, E // 2) as ee:
                    for k in range(2):
                        pool.wait_ge(s["slot"], b * E + ee * 2 + k + 1)
                        plain(pool)
                        pool.tensor_copy(W13S[k][:, :], W13T[:, ee * 2 + k, :])
                        pool.tensor_copy(W2S[k][:, :], W2T[:, ee * 2 + k, :]).then_inc(s["wcopy"], 1)

        @block.scalar
        def _(act):
            act.wait_ge(s["wmodld"], 32)
            act.activation(csil[:, :], cs[:, :], ACT.Silu).then_inc(s["csil"], 1)
            act.wait_ge(s["small"], 16 * 15)
            with act.Fori(0, B) as b:
                act.preload_act_table_set("natural_log_exp_and_others")
                def inverse_root(k):
                    act.wait_ge(s["var"], b * 4 + k + 1)
                    act.activation(st[:, 3, :], st[:, 2, :], ACT.Ln).then_inc(s["r0"], 1)
                    act.wait_ge(s["r0"], b * 8 + 2 * k + 1)
                    act.activation(st[:, 4, :], st[:, 3, :], ACT.Exp, scale=-0.5).then_inc(s["r0"], 1)

                def exps(p, c, kt):
                    D = b * DUOS + p * NC + c
                    act.wait_ge(s["main"], 1 + D * STEPS + kt + 1)
                    if kt >= 4:
                        act.wait_ge(s["pv"], D * STEPS + kt - 3)
                    act.wait_ge(s["sum"], 4 + D * ADDS + (max(1, kt - 4) if kt >= 4 else kt - 3))
                    act.activation(buf1(kt), SC[:, kt % 2, :], ACT.Exp, scale=DK ** -0.5).then_inc(s["exp"], 1)

                def q_out(p, c):
                    D = b * DUOS + p * NC + c
                    act.wait_ge(s["q"], 1 + D + 1)
                    act.wait_ge(s["qs"], 1 + 2 * D)
                    act.wait_ge(s["q2"], 1 + D)
                    plain(act)
                    act.activation(QF[:, :], XP[:, :], ACT.Identity, bias=bqs[:, bass.ds(p, 1)]).then_inc(s["qf"], 1)

                def q_fill(p, c):
                    act.wait_ge(s["qf"], b * DUOS + p * NC + c + 1)
                    act.activation(Q2[c][0:64, 0:CH], QF[0:64, :], ACT.Copy)
                    act.activation(Q2[c][0:64, CH:2 * CH], QF[64:128, :], ACT.Copy).then_inc(s["q2"], 1)

                def inverse(p, c):
                    D = b * DUOS + p * NC + c
                    act.wait_ge(s["den"], D + 1)
                    act.activation(LD[:, :], XP[:, :], ACT.Ln).then_inc(s["rd"], 1)
                    act.wait_ge(s["rd"], D * 2 + 1)
                    act.activation(RD[:, :], LD[:, :], ACT.Exp, scale=-1.0).then_inc(s["rd"], 1)

                def duo_acts(p, c, first, last):
                    D = b * DUOS + p * NC + c
                    for kt in (1, 2, 3):
                        exps(p, c, kt)
                    if not last:
                        q_out(*after(p, c, 2))
                    exps(p, c, 4)
                    if not (first and c == 0):
                        inverse(*after(p, c, -1))
                    for kt in (5, 6, 7):
                        exps(p, c, kt)
                    if not last:
                        q_fill(*after(p, c, 2))
                    if not (last and c == 1):
                        exps(*after(p, c, 1), 0)
                    act.wait_ge(s["pv"], D * STEPS + STEPS)
                    act.wait_ge(s["norm"], 1 + D)
                    act.activation(OE[:, :], PV[:, :], ACT.Copy).then_inc(s["pve"], 1)

                inverse_root(0)
                act.wait_ge(s["hT"], b + 1)
                act.activation(HT[:, :], SC[:, 0, :], ACT.Copy).then_inc(s["hTc"], 1)
                for c in range(NC):
                    q_out(0, c)
                    q_fill(0, c)
                exps(0, 0, 0)
                for c in range(NC):
                    duo_acts(0, c, True, False)
                with act.Fori(1, PAIRS - 1) as p:
                    for c in range(NC):
                        duo_acts(p, c, False, False)
                for c in range(NC):
                    duo_acts(PAIRS - 1, c, False, True)
                inverse(PAIRS - 1, NC - 1)
                act.wait_ge(s["op"], 1 + b + 1)
                act.activation(TA[:, :, :].rearrange("p t d -> p (t d)"), SC[:, 0, :], ACT.Identity, bias=bos[:, 0:1]).then_inc(s["opc"], 1)
                inverse_root(1)
                inverse_root(2)
                act.wait_ge(s["h3T"], b + 1)
                act.activation(HT[:, :], SC[:, 0, :], ACT.Copy).then_inc(s["h3Tc"], 1)
                act.wait_ge(s["qkv"], b + 1)
                act.activation(qkv[:, :, :], SCF.rearrange("p (t n) -> p t n", t=NT)[:, :, 0:QKV], ACT.Copy).then_inc(s["qkvc"], 1)
                act.wait_ge(s["kT"], b + 1)
                for g in range(NG):
                    last = act.activation(KT[32 * g:32 * g + 32, g, :], SC[32 * g:32 * g + 32, 0, :], ACT.Copy)
                last.then_inc(s["kTc"], 1)

                def q_turned(J):
                    act.wait_ge(s["ta"], J + 1)
                    act.activation(QTA[:, :], MX[:, :], ACT.Copy).then_inc(s["qta"], 1)

                def q_with_max(j):
                    act.wait_ge(s["tb"], 2 + b * HPG + j)
                    act.activation(QTB[:, j, :], MX[:, :], ACT.Copy).then_inc(s["qtb"], 1)

                def heads_of(j, last):
                    J = b * HPG + j
                    n = 0
                    for c in range(NC):
                        for kt in range(4 * c + 4):
                            off, cnt = rows((c, kt))
                            pvi = 4 * c + kt
                            for hh in range(2):
                                act.wait_ge(s["main2"], J * ST2 + n + 1)
                                if pvi >= 2:
                                    act.wait_ge(s["pv2"], J * PV2 + pvi - 1)
                                act.activation(P[:, pvi % 2, 2 * hh:2 * hh + 2, off:CH],
                                               SC[:, n % 2, :].rearrange("p (g q) -> p g q", g=2)[:, :, off:CH],
                                               ACT.Exp, scale=HD ** -0.5).then_inc(s["exp2"], 1)
                                n += 1
                            if pvi == 1 and c == 0 and not last:
                                q_turned(J + 1)
                        act.wait_ge(s["pv2"], J * PV2 + pvi + 1)
                        act.wait_ge(s["ovt"], 1 + J * 2 + c)
                        act.activation(OV[:, :], PV[:, :], ACT.Copy).then_inc(s["ov"], 1)
                    if not last:
                        q_with_max(j + 1)

                q_turned(b * HPG)
                q_with_max(0)
                with act.Fori(0, HPG - 1) as j:
                    heads_of(j, False)
                heads_of(HPG - 1, True)
                act.wait_ge(s["aoT"], b + 1)
                act.activation(HT[:, :], SC[:, 0, :], ACT.Copy).then_inc(s["aoTc"], 1)
                inverse_root(3)
                act.wait_ge(s["h4T"], 1 + b + 1)
                act.activation(HT[:, :], SC[:, 0, :], ACT.Copy).then_inc(s["h4Tc"], 1)
                act.wait_ge(s["lg"], b * 2 + 2)
                act.activation(W8[:, :, :], L8[:, :, :], ACT.Exp).then_inc(s["rt"], 1)
                with act.Fori(0, E // 2) as ee:
                    for k in range(2):
                        for t in range(4):
                            act.wait_ge(s["up"], (b * E + ee * 2 + k) * 4 + t + 1)
                            act.activation(SG[:, t % 2, :], SC[:, t % 2, 0:CH], ACT.Silu).then_inc(s["silu"], 1)

        @block.vector
        def _(dve):
            link0 = Chain(dve, s["one"])
            link = link0.link
            dve.memset(KL[:, :].bitcast(F32), 0.0).then_inc(s["const"], 1)
            dve.memset(ones[:, :], 1.0).then_inc(s["const"], 1)
            dve.memset(Q2[0][:, :].bitcast(F32), 0.0).then_inc(s["const"], 1)
            dve.memset(Q2[1][:, :].bitcast(F32), 0.0).then_inc(s["const"], 1)
            dve.memset(KT[:, :, :].bitcast(F32), 0.0).then_inc(s["const"], 1)
            dve.memset(QSJ[:, :, :, :].bitcast(F32), 0.0).then_inc(s["const"], 1)
            dve.memset(V2[:, :, :, :], 0.0).then_inc(s["const"], 1)
            dve.memset(M2[:, :, :, :], LOW).then_inc(s["const"], 1)
            dve.wait_ge(s["const"], 8)
            dve.memset(KL[64:65, :].bitcast(F32), 1.0).then_inc(s["const"], 1)
            dve.memset(V2[:, :, :, HD:2 * HD], 1.0).then_inc(s["const"], 1)
            dve.wait_ge(s["csil"], 1)
            for b in range(B):
                last = dve.tensor_copy(cbc[:, b, :], csil[:, b:b + 1].to_broadcast([128, 128]))
            last.then_inc(s["cbc"], 1)
            dve.wait_ge(s["mod"], 1)
            for b in range(B):
                last = dve.tensor_copy(mods[:, b, 0:3, :], MX[:, 0:384].rearrange("p (k d) -> p k d", k=3)) if b == 0 else \
                    dve.tensor_copy(mods[:, b, 0:3, :], PV[:, 0:384].rearrange("p (k d) -> p k d", k=3))
                last = dve.tensor_copy(mods[:, b, 3:6, :], MX[:, 512:896].rearrange("p (k d) -> p k d", k=3)) if b == 0 else \
                    dve.tensor_copy(mods[:, b, 3:6, :], XP[:, 0:384].rearrange("p (k d) -> p k d", k=3))
            link(last)
            for b in range(B):
                for k in (1, 4):
                    link(dve.tensor_scalar(mods[:, b, k, :], mods[:, b, k, :], 1.0, None, ALU.add))
                for k in (2, 5):
                    link(dve.tensor_scalar(gsgn[:, :], mods[:, b, k, :], 0.0, 2.0, ALU.is_ge, ALU.mult))
                    link(dve.scalar_tensor_tensor(out=mods[:, b, k, :], in0=gsgn[:, :], scalar=1.0,
                                                  in1=mods[:, b, k, :], op0=ALU.subtract, op1=ALU.mult))
                    link(dve.tensor_scalar(mods[:, b, k, :], mods[:, b, k, :], 0.25, None, ALU.max))
                    link(dve.scalar_tensor_tensor(out=mods[:, b, k, :], in0=gsgn[:, :], scalar=1.0,
                                                  in1=mods[:, b, k, :], op0=ALU.subtract, op1=ALU.mult))
            dve.wait_ge(s["small"], 16 * 15)
            dve.wait_ge(s["io"], 1)
            dve.wait_ge(s["tri"], 1)
            with dve.Fori(0, B) as b:
                ch = Chain(dve, s["dve"])
                ch.base = b * DVE_STEPS
                link = ch.link

                def tt(o, x, y, op):
                    return dve.tensor_tensor(o, x, y, op)

                def inverse_root(k):
                    dve.wait_ge(s["r0"], b * 8 + 2 * k + 2)
                    link(tt(st[:, 5, :], st[:, 4, :], st[:, 4, :], ALU.mult))
                    link(tt(st[:, 5, :], st[:, 5, :], st[:, 2, :], ALU.mult))
                    link(dve.tensor_scalar(st[:, 5, :], st[:, 5, :], -0.5, 1.5, ALU.mult, ALU.add))
                    link(tt(st[:, 5, :], st[:, 5, :], st[:, 4, :], ALU.mult))

                def mean_square(x, k):
                    link(tt(TB[:, :, :], x, x, ALU.mult))
                    link(dve.tensor_reduce(st[:, 1, :], TB[:, :, :], AX_X, ALU.add))
                    dve.tensor_scalar(st[:, 2, :], st[:, 1, :], 1.0 / D, EPS, ALU.mult, ALU.add).then_inc(s["var"], 1)

                def layer_norm(x, o, k, shift, scale):
                    link(dve.tensor_reduce(st[:, 0, :], x, AX_X, ALU.add))
                    link(dve.tensor_scalar(st[:, 0, :], st[:, 0, :], -1.0 / D, None, ALU.mult))
                    link(tt(o, x, per_token(st[:, 0, :]), ALU.add))
                    mean_square(o, k)
                    inverse_root(k)
                    link(tt(o, o, per_token(st[:, 5, :]), ALU.mult))
                    link(tt(o, o, bc(scale), ALU.mult))
                    return tt(o, o, bc(shift), ALU.add)

                def rms_norm(x, o, k, weight):
                    mean_square(x, k)
                    inverse_root(k)
                    link(tt(o, x, per_token(st[:, 5, :]), ALU.mult))
                    return tt(o, o, bc(weight), ALU.mult)

                dve.wait_ge(s["xld"], b * 16 + 16)
                dve.wait_ge(s["h4T"], 1 + b)
                layer_norm(X[:, :, :], HA[:, :, :], 0, mods[:, b, 0, :], mods[:, b, 1, :]).then_inc(s["h"], 1)
                dve.wait_ge(s["kv"], b + 1)
                link(dve.tensor_scalar(KK[:, :], SC[:, 1, :], bks[:, 0:1], None, ALU.add))
                dve.scalar_tensor_tensor(out=KL[0:64, :], in0=SC[0:64, 1, :], scalar=bks[0:64, 0:1],
                                         in1=KK[0:64, :].bitcast(F32), op0=ALU.add, op1=ALU.subtract)
                tt(V1[:, :, 0:DK], MX[:, 0:CH].rearrange("p (t d) -> p t d", d=DK), bc(bvs[:, :]), ALU.add).then_inc(s["kvx"], 1)

                def split(p, c, first=False):
                    D = b * DUOS + p * NC + c
                    dve.wait_ge(s["qf"], D + 1)
                    if not first:
                        dve.wait_ge(s["main"], 1 + (D - 1) * STEPS)
                    for h in range(2):
                        src = QF[64 * h:64 * h + 64, :]
                        hi, lo = QS[c][h][64 * h:64 * h + 64, :], QS[c][h][64 - 64 * h:128 - 64 * h, :]
                        link(dve.tensor_copy(hi, src))
                        tt(lo, src, hi.bitcast(F32), ALU.subtract).then_inc(s["qs"], 1)

                def max_of(p, c, i, alone=False):
                    D = b * DUOS + p * NC + c
                    dve.wait_ge(s["mx"], D * MAXES + i + 1)
                    if i == 0:
                        dve.wait_ge(s["mt"], 1 + D)
                    dve.tensor_reduce(MC[:, i:i + 1], max_place(i, alone), AX_X, ALU.max, negate=True).then_inc(s["mred"], 1)

                def max_out(p, c):
                    D = b * DUOS + p * NC + c
                    dve.wait_ge(s["mt"], 1 + D + 1)
                    dve.wait_ge(s["mdma"], 16 + D * 16)
                    dve.tensor_copy(MR[:, :], XP[0:MAXES, 0:128]).then_inc(s["mrow"], 1)

                def norm(p, c, part):
                    D = b * DUOS + p * NC + c
                    if part == 0:
                        dve.wait_ge(s["rd"], D * 2 + 2)
                        tt(LD[:, :], XP[:, :], RD[:, :], ALU.mult).then_inc(s["n0"], 1)
                    elif part == 1:
                        dve.wait_ge(s["n0"], D + 1)
                        link(dve.scalar_tensor_tensor(out=RD[:, :], in0=LD[:, :], scalar=2.0, in1=RD[:, :],
                                                      op0=ALU.subtract, op1=ALU.mult))
                    else:
                        dve.wait_ge(s["pve"], 1 + D + 1)
                        dve.scalar_tensor_tensor(out=AT[:, p, c * CH:(c + 1) * CH], in0=OE[:, :], scalar=-1.0,
                                                 in1=RD[:, :], op0=ALU.mult, op1=ALU.mult).then_inc(s["norm"], 1)

                def duo_ops(p, c, first, last):
                    before = not (first and c == 0)
                    one, two = not (last and c == 1), not last
                    prev, nxt, nxt2 = after(p, c, -1), after(p, c, 1), after(p, c, 2)
                    if one:
                        max_of(*nxt, 1)
                    if one:
                        for i in range(2, 7):
                            max_of(*nxt, i)
                    if before:
                        norm(*prev, 0)
                    if one:
                        max_of(*nxt, 7)
                    if before:
                        norm(*prev, 1)
                    if one:
                        max_out(*nxt)
                    if before:
                        norm(*prev, 2)
                    if two:
                        split(*nxt2)
                        max_of(*nxt2, 0)

                dve.wait_ge(s["op"], 1 + b)
                split(0, 0, first=True)
                split(0, 1, first=True)
                for i in range(MAXES):
                    max_of(0, 0, i, alone=True)
                max_out(0, 0)
                max_of(0, 1, 0)
                for c in range(NC):
                    duo_ops(0, c, True, False)
                n0 = ch.n
                with dve.Fori(1, PAIRS - 1) as p:
                    ch.base = b * DVE_STEPS + (p - 1) * DVE_PAIR
                    for c in range(NC):
                        duo_ops(p, c, False, False)
                    got = ch.n - n0
                assert got == DVE_PAIR, got
                ch.base = b * DVE_STEPS
                ch.n = n0 + (PAIRS - 2) * DVE_PAIR
                for c in range(NC):
                    duo_ops(PAIRS - 1, c, False, True)
                for part in range(3):
                    norm(PAIRS - 1, NC - 1, part)

                dve.wait_ge(s["opT"], b + 1)
                link(tt(X1[:, :, :], tiles(SC[:, 1, :]), bc(mods[:, b, 2, :]), ALU.mult))
                link(tt(X1[:, :, :], X1[:, :, :], X[:, :, :], ALU.add))
                dve.sem_inc(s["x1"], 1)
                link(layer_norm(X1[:, :, :], H2[:, :, :], 1, mods[:, b, 3, :], mods[:, b, 4, :]))
                rms_norm(H2[:, :, :], HA[:, :, :], 2, lns[:, 0, :]).then_inc(s["h3"], 1)

                dve.wait_ge(s["qkvc"], b + 1)
                nqk = QKV - NG * HD
                half = HD // 2
                q4 = qkv[:, :, 0:nqk].rearrange("p t (h d) -> p t h d", d=HD)
                r4 = qkr[:, :, :].rearrange("p t (h d) -> p t h d", d=HD)
                o4 = qko[:, :, :].rearrange("p t (h d) -> p t h d", d=HD)

                def per_head(ap):
                    return ap.unsqueeze(2).to_broadcast([128, NT, nqk // HD, ap.shape[-1]])

                tt(r4[:, :, :, 0:half], q4[:, :, :, half:HD], per_head(ropes[:, :, 1, 0:half]), ALU.mult)
                tt(r4[:, :, :, half:HD], q4[:, :, :, 0:half], per_head(ropes[:, :, 1, half:HD]), ALU.mult)
                link(tt(o4, q4, per_head(ropes[:, :, 0, :]), ALU.mult))
                link(tt(qkr[:, :, :], qkr[:, :, :], qko[:, :, :], ALU.add))
                dve.tensor_copy(V2[:, :, :, 0:HD], qkv[:, :, nqk:QKV].rearrange("p t (g d) -> p t g d", g=NG)).then_inc(s["vset"], 1)
                k4 = qkr[:, :, 128:nqk].rearrange("p t (g d) -> p t g d", g=NG)
                link(dve.tensor_copy(KS[:, :, :, 0:8], k4))
                dve.tensor_copy(KS[:, :, :, 8:16], k4)
                tt(KS[:, :, :, 16:24], k4, KS[:, :, :, 0:8].bitcast(F32), ALU.subtract)
                dve.memset(KS[:, :, :, MROW:MROW + 1].bitcast(F32), 1.0).then_inc(s["ks"], 1)
                dve.wait_ge(s["kT"], b + 1)
                plain(dve)

                def stack_q(j):
                    J = b * HPG + j
                    q4 = qkr[:, :, 0:128].rearrange("p t (g j d) -> p j t g d", g=NG, j=HPG)[:, j]
                    dve.wait_ge(s["tb"], 1 + J)
                    plain(dve)
                    link(dve.tensor_copy(QSJ[:, :, :, 0:8], q4))
                    plain(dve)
                    dve.tensor_copy(QSJ[:, :, :, 16:24], q4)
                    dve.memset(QSJ[:, :, :, MROW:MROW + 1].bitcast(F32), 0.0)
                    tt(QSJ[:, :, :, 8:16], q4, QSJ[:, :, :, 0:8].bitcast(F32), ALU.subtract).then_inc(s["qsj"], 1)

                def reduce_pieces(J, step):
                    for t, g, piece, k0, w in pieces(step):
                        i = item(t, g, piece)
                        dve.wait_ge(s["m2"], J * ITEMS + i + 1)
                        if i >= 4:
                            dve.wait_ge(s["m2red"], J * ITEMS + i - 2)
                        plain(dve)
                        src = max_bank(i, step is None, w)
                        if piece:
                            ins = dve.tensor_tensor_reduce(out=junk[:, i % 4, 0:w], in0=src, in1=tri[:, CH - w:CH], scale=1.0,
                                                           scalar=-3.0e38, op0=ALU.add, op1=ALU.max, accum_out=M2[:, t, g, 0:1])
                        else:
                            ins = dve.tensor_reduce(M2[:, t, g, 1:2], src, AX_X, ALU.max)
                        ins.then_inc(s["m2red"], 1)

                def stack_max(J):
                    dve.wait_ge(s["m2red"], 1 + J * ITEMS + ITEMS)
                    dve.tensor_reduce(QSJ[:, :, :, MROW:MROW + 1], M2[:, :, :, :], AX_X, ALU.max, negate=True).then_inc(s["qsm"], 1)

                def divide(j, c):
                    J = b * HPG + j
                    dve.wait_ge(s["ovt"], 1 + J * 2 + c + 1)
                    x4 = XP[:, :].rearrange("p (t g r) -> p t g r", t=4, g=NG)
                    link(dve.reciprocal(RC[:, :, :], x4[:, :, :, HD]))
                    link(tt(AO[:, 4 * c:4 * c + 4, :].rearrange("p t (g j d) -> p j t g d", g=NG, j=HPG)[:, j],
                            x4[:, :, :, 0:HD], RC[:, :, :].unsqueeze(3).to_broadcast([128, 4, NG, HD]), ALU.mult))
                    dve.sem_inc(s["ao"], 1)

                def heads_of(j, last):
                    if not last:
                        stack_q(j + 1)
                    for step in range(PV2):
                        if not last:
                            reduce_pieces(b * HPG + j + 1, step)
                        if step == 6:
                            divide(j, 0)
                    if not last:
                        stack_max(b * HPG + j + 1)
                    divide(j, 1)

                stack_q(0)
                reduce_pieces(b * HPG, None)
                stack_max(b * HPG)
                n0 = ch.n
                with dve.Fori(0, HPG - 1) as j:
                    ch.base = b * DVE_STEPS + j * DVE_J
                    heads_of(j, False)
                    got = ch.n - n0
                assert got == DVE_J, got
                ch.base = b * DVE_STEPS
                ch.n = n0 + (HPG - 1) * DVE_J
                heads_of(HPG - 1, True)

                dve.wait_ge(s["wo2"], b + 1)
                link(tt(H2[:, :, :], tiles(SC[:, 1, :]), H2[:, :, :], ALU.add))
                rms_norm(H2[:, :, :], HA[:, :, :], 3, lns[:, 1, :]).then_inc(s["h4"], 1)
                dve.wait_ge(s["lg"], b * 2 + 1)
                link(dve.tensor_copy(L8[:, :, :], XP[:, 0:NT * E].rearrange("p (t e) -> p t e", e=E)))
                plain(dve)
                for t in range(NT):
                    last = dve.max(T8[:, t, :], L8[:, t, :])
                link(last)
                plain(dve)
                for t in range(NT):
                    last = dve.max_index(I8[:, t, :], T8[:, t, :], L8[:, t, :])
                link(last)
                link(tt(L8[:, :, :], L8[:, :, :], T8[:, :, 0:1].to_broadcast([128, NT, E]), ALU.subtract))
                dve.sem_inc(s["lg"], 1)
                link(dve.tensor_copy(IF[:, :, :], I8[:, :, 0:2]))
                link(tt(WF[:, :, :], bc(io8[:, :]), IF[:, :, 0:1].to_broadcast([128, NT, E]), ALU.is_equal))
                link(tt(T8[:, :, :], bc(io8[:, :]), IF[:, :, 1:2].to_broadcast([128, NT, E]), ALU.is_equal))
                link(tt(WF[:, :, :], WF[:, :, :], T8[:, :, :], ALU.add))
                dve.wait_ge(s["rt"], b + 1)
                link(tt(WF[:, :, :], WF[:, :, :], W8[:, :, :], ALU.mult))
                link(dve.tensor_reduce(st[:, 6, :], WF[:, :, :], AX_X, ALU.add))
                link(dve.reciprocal(st[:, 7, :], st[:, 6, :]))
                link(tt(WF[:, :, :], WF[:, :, :], per_token(st[:, 7, :], E), ALU.mult))
                link(dve.memset(ACC[:, :, :], 0.0))
                dve.wait_ge(s["out"], 16 + b * 16)
                plain(dve)

                def gated(e, t):
                    dve.wait_ge(s["silu"], (b * E + e) * 4 + t + 1)
                    tt(G[:, t // 2, t % 2, :], SG[:, t % 2, :], SC[:, t % 2, CH:2 * CH], ALU.mult).then_inc(s["g"], 1)

                def accumulate(e, c):
                    n = b * E + e
                    if c == 0:
                        dve.wait_ge(s["down"], n + 1)
                        dve.wait_ge(s["mods"], 1 + n * 2)
                    else:
                        dve.wait_ge(s["slot"], n + 3)
                    plain(dve)
                    tt(TA[:, 4 * c:4 * c + 4, :], tiles(MX[:, c * CH:(c + 1) * CH]),
                       WF[:, 4 * c:4 * c + 4, bass.ds(e, 1)].to_broadcast([128, 4, D]), ALU.mult).then_inc(s["accfree"], 1)
                    dve.wait_ge(s["accfree"], n * 2 + c + 3)
                    tt(ACC[:, 4 * c:4 * c + 4, :], ACC[:, 4 * c:4 * c + 4, :], TA[:, 4 * c:4 * c + 4, :], ALU.add).then_inc(s["mods"], 1)

                def expert(e, last):
                    for t in (1, 2, 3):
                        gated(e, t)
                    accumulate(e, 0)
                    if not last:
                        gated(e + 1, 0)
                    accumulate(e, 1)

                gated(0, 0)
                with dve.Fori(0, E // 2 - 1) as ee:
                    for k in range(2):
                        expert(ee * 2 + k, False)
                for e in (E - 2, E - 1):
                    expert(e, e == E - 1)
                dve.wait_ge(s["mods"], 1 + b * (2 * E) + 2 * E)
                link(tt(TA[:, :, :], ACC[:, :, :], H2[:, :, :], ALU.add))
                link(tt(TA[:, :, :], TA[:, :, :], bc(mods[:, b, 5, :]), ALU.mult))
                tt(TA[:, :, :], TA[:, :, :], X1[:, :, :], ALU.add).then_inc(s["y"], 1)
                assert ch.n == DVE_STEPS, ch.n

        @block.tensor
        def _(pe):
            mm = pe.matmul
            pe.wait_ge(s["idn"], 3)
            pe.wait_ge(s["wmodld"], 32)
            pe.wait_ge(s["const"], 10)
            pe.wait_ge(s["cbc"], 1)
            for o, b, c in ((MX[:, 0:384], 0, 0), (MX[:, 512:896], 0, 1), (PV[:, 0:384], 1, 0), (XP[:, 0:384], 1, 1)):
                last = mm(o, cbc[:, b, :], wmods[:, c * 384:(c + 1) * 384], start=True, stop=True)
            last.then_inc(s["mod"], 1)
            pe.wait_ge(s["small"], 16 * 15)
            pe.wait_ge(s["one"], 21)
            with pe.Fori(0, B) as b:
                def transposes(src, half):
                    for t in range(NT):
                        last = pe.transpose(SC[:, half, t * 128:t * 128 + 128], src[:, t, :], ident[:, :])
                    return last

                pe.wait_ge(s["h"], b + 1)
                transposes(HA, 0).then_inc(s["hT"], 1)
                pe.wait_ge(s["hTc"], b + 1)
                for c in range(NC):
                    mm(SC[:, 1, c * CH:(c + 1) * CH], wk2[:, :], HT[:, c * CH:(c + 1) * CH], start=True, stop=True)
                for t in range(NT):
                    last = mm(MX[:, t * DK:(t + 1) * DK], HT[:, t * 128:(t + 1) * 128], wvs[:, :], start=True, stop=True)
                last.then_inc(s["kv"], 1)

                def q_proj(p, c):
                    D = b * DUOS + p * NC + c
                    pe.wait_ge(s["wqld"], (b * PAIRS + p) * 16 + 16)
                    if isinstance(p, int) and p == 0 and c == 1:
                        pe.wait_ge(s["qf"], D)
                    elif isinstance(p, int) and p == 0:
                        pe.wait_ge(s["mrow"], 1 + D)
                    else:
                        pe.wait_ge(s["mrow"], D)
                    mm(XP[:, :], wqs[:, :], HT[:, c * CH:(c + 1) * CH], start=True, stop=True).then_inc(s["q"], 1)

                def max_pass(p, c, i, alone=False):
                    D = b * DUOS + p * NC + c
                    h, t = i // 4, i % 4
                    if t == 0:
                        pe.wait_ge(s["qs"], 1 + 2 * D + h + 1)
                    pe.wait_ge(s["mred"], 1 + D * MAXES + (max(0, i - 2) if alone else i))
                    q = QS[c][h][:, t * 128:(t + 1) * 128]
                    o = max_place(i, alone)
                    mm(o[:, 0:CH], q, KK[:, 0:CH], start=True, stop=True)
                    mm(o[:, CH:S], q, KK[:, CH:S], start=True, stop=True).then_inc(s["mx"], 1)

                def max_turn(p, c, begun, before=False):
                    D = b * DUOS + p * NC + c
                    pe.wait_ge(s["mred"], 1 + D * MAXES + MAXES)
                    pe.wait_ge(s["qf"], D + begun)
                    pe.wait_ge(s["mrow"], 1 + D)
                    if before:
                        pe.wait_ge(s["n0"], D - 1)
                    pe.transpose(XP[0:MAXES, 0:128], MC[:, :], ident[:, :]).then_inc(s["mt"], 1)

                def scores(p, c, kt, *parts):
                    D = b * DUOS + p * NC + c
                    for part in parts:
                        h = part % 2
                        o = SC[:, kt % 2, h * CH:(h + 1) * CH]
                        if kt >= 2 and part == 0:
                            pe.wait_ge(s["exp"], D * STEPS + kt - 1)
                        if kt == 0 and part == 2:
                            pe.wait_ge(s["mdma"], 16 + D * 16 + 16)
                            pe.wait_ge(s["q2"], 1 + D + 1)
                        if part < 2:
                            mm(o, KK[:, kt * 128:(kt + 1) * 128], QS[c][h], start=True, stop=False)
                        else:
                            last = mm(o, KL[:, kt * 128:(kt + 1) * 128], Q2[c][:, h * CH:(h + 1) * CH], start=False, stop=True)
                        if part == 3:
                            last.then_inc(s["main"], 1)

                def weigh(p, c, kt):
                    D = b * DUOS + p * NC + c
                    pe.wait_ge(s["exp"], D * STEPS + kt + 1)
                    if kt == 0:
                        pe.wait_ge(s["pve"], 1 + D)
                    for h in range(2):
                        last = mm(PV[64 * h:64 * h + 64, :], V1[:, kt, :], buf1(kt)[:, h * CH:(h + 1) * CH],
                                  start=(kt == 0), stop=(kt == NT - 1))
                    last.then_inc(s["pv"], 1)

                def denominators(p, c, begun):
                    D = b * DUOS + p * NC + c
                    pe.wait_ge(s["sum"], 4 + D * ADDS + ADDS)
                    pe.wait_ge(s["qf"], D + begun)
                    for h in range(2):
                        last = mm(XP[64 * h:64 * h + 64, :], ones[:, :], TS[c][:, h * CH:(h + 1) * CH], start=True, stop=True)
                    last.then_inc(s["den"], 1)

                def duo_mms(p, c, first, last):
                    before = not (first and c == 0)
                    one, two = not (last and c == 1), not last
                    nxt, nxt2 = after(p, c, 1), after(p, c, 2)

                    def maxima(i):
                        if one:
                            max_pass(*nxt, i)

                    scores(p, c, 1, 0)
                    maxima(1)
                    scores(p, c, 1, 1, 2, 3)
                    weigh(p, c, 0)
                    maxima(2)
                    scores(p, c, 2, 0, 1)
                    weigh(p, c, 1)
                    scores(p, c, 2, 2)
                    maxima(3)
                    scores(p, c, 2, 3)
                    scores(p, c, 3, 0, 1, 2, 3)
                    if two:
                        q_proj(*nxt2)
                    maxima(4)
                    weigh(p, c, 2)
                    scores(p, c, 4, 0, 1, 2)
                    maxima(5)
                    scores(p, c, 4, 3)
                    weigh(p, c, 3)
                    scores(p, c, 5, 0, 1)
                    maxima(6)
                    scores(p, c, 5, 2, 3)
                    if before:
                        denominators(*after(p, c, -1), 4 if two else 3 - c)
                    weigh(p, c, 4)
                    maxima(7)
                    scores(p, c, 6, 0, 1, 2, 3)
                    weigh(p, c, 5)
                    if one:
                        max_turn(*nxt, 2 if two else 1, before)
                    scores(p, c, 7, 0, 1, 2, 3)
                    weigh(p, c, 6)
                    if one:
                        scores(*nxt, 0, 0, 1)
                    if two:
                        max_pass(*nxt2, 0)
                    weigh(p, c, 7)
                    if one:
                        scores(*nxt, 0, 2, 3)

                q_proj(0, 0)
                q_proj(0, 1)
                pe.wait_ge(s["kvx"], b + 1)
                for i in range(MAXES):
                    max_pass(0, 0, i, alone=True)
                max_turn(0, 0, 2)
                scores(0, 0, 0, 0, 1)
                max_pass(0, 1, 0)
                scores(0, 0, 0, 2, 3)
                for c in range(NC):
                    duo_mms(0, c, True, False)
                with pe.Fori(1, PAIRS - 1) as p:
                    for c in range(NC):
                        duo_mms(p, c, False, False)
                for c in range(NC):
                    duo_mms(PAIRS - 1, c, False, True)
                pe.wait_ge(s["n0"], b * DUOS + DUOS - 1)
                denominators(PAIRS - 1, NC - 1, 1)
                pe.wait_ge(s["norm"], 1 + b * DUOS + DUOS)
                for c in range(NC):
                    for p in range(PAIRS):
                        last = mm(SC[:, 0, c * CH:(c + 1) * CH], wos[:, p, :], AT[:, p, c * CH:(c + 1) * CH],
                                  start=(p == 0), stop=(p == PAIRS - 1))
                last.then_inc(s["op"], 1)
                pe.wait_ge(s["opc"], b + 1)
                transposes(TA, 1).then_inc(s["opT"], 1)
                pe.wait_ge(s["h3"], b + 1)
                transposes(HA, 0).then_inc(s["h3T"], 1)
                pe.wait_ge(s["h3Tc"], b + 1)
                for t in range(NT):
                    last = mm(SCF[:, t * 256:t * 256 + QKV], HT[:, t * 128:(t + 1) * 128], WQKVT[:, 0:QKV], start=True, stop=True)
                last.then_inc(s["qkv"], 1)
                pe.wait_ge(s["ks"], b + 1)
                pe.wait_ge(s["qkvc"], b + 1)

                def turn_stack(o):
                    for t in range(NT):
                        last = pe.transpose(o[:, t * 128:t * 128 + 128], QSJ[:, t, :, :].rearrange("p g r -> p (g r)").bitcast(F32), ident[:, :])
                    return last

                turn_stack(SC[:, 0, :]).then_inc(s["kT"], 1)
                pe.wait_ge(s["kTc"], b + 1)
                pe.wait_ge(s["vset"], b + 1)

                def max_pieces(J, step, first=0, end=ITEMS):
                    for t, g, piece, k0, w in pieces(step)[first:end]:
                        i = item(t, g, piece)
                        if i == 0:
                            pe.wait_ge(s["qta"], J + 1)
                        pe.wait_ge(s["m2red"], 1 + J * ITEMS + max(0, i - (5 if step is None else 1)))
                        mm(max_bank(i, step is None, w), QTA[:, t * 128:(t + 1) * 128], KT[:, g, k0:k0 + w],
                           start=True, stop=True).then_inc(s["m2"], 1)

                def turn_q(J):
                    pe.wait_ge(s["qsj"], J + 1)
                    turn_stack(MX).then_inc(s["ta"], 1)

                def turn_q_with_max(J):
                    pe.wait_ge(s["qsm"], J + 1)
                    turn_stack(MX).then_inc(s["tb"], 1)

                def heads_of(j, last):
                    J = b * HPG + j
                    pe.wait_ge(s["qtb"], J + 1)
                    if last:
                        plain(pe)

                    def weigh2(c, kt):
                        off, cnt = rows((c, kt))
                        pvi = 4 * c + kt
                        pe.wait_ge(s["exp2"], J * ST2 + (8 if c else 0) + 2 * kt + 2)
                        if kt >= 4 * c:
                            pe.wait_ge(s["tri2"], J * 16 + 8 * c + 2 * (kt - 4 * c) + 2)
                        if kt == 0:
                            pe.wait_ge(s["ov"], 1 + J * 2 + c)
                        for g in range(NG):
                            last = mm(PV[32 * g:32 * g + 32, off:CH], V2[:, kt, g, :], P[:, pvi % 2, g, off:CH],
                                      start=(kt == 0), stop=(kt == 4 * c + 3))
                        last.then_inc(s["pv2"], 1)

                    def turn_out(c):
                        pe.wait_ge(s["ov"], 1 + J * 2 + c + 1)
                        pe.wait_ge(s["ao"], 1 + J * 2 + c)
                        for t in range(4):
                            last = pe.transpose(XP[:, t * 128:(t + 1) * 128], OV[:, t * 128:(t + 1) * 128], ident[:, :])
                        last.then_inc(s["ovt"], 1)

                    n = 0
                    for c in range(NC):
                        for kt in range(4 * c + 4):
                            off, cnt = rows((c, kt))
                            step = 4 * c + kt
                            for hh in range(2):
                                if n >= 2:
                                    pe.wait_ge(s["exp2"], J * ST2 + n - 1)
                                for g in (2 * hh, 2 * hh + 1):
                                    mn = mm(SC[:, n % 2, (g % 2) * CH + off:(g % 2) * CH + CH], KT[:, g, kt * 128:(kt + 1) * 128],
                                            QTB[:, j, c * CH + off:(c + 1) * CH], start=True, stop=True)
                                mn.then_inc(s["main2"], 1)
                                n += 1
                                if not last:
                                    max_pieces(J + 1, step, 2 * hh, 2 + hh)
                            if step == 1 and not last:
                                turn_q(J + 1)
                            if kt > 0:
                                weigh2(c, kt - 1)
                            elif c == 1:
                                weigh2(0, 3)
                            if not last:
                                max_pieces(J + 1, step, 3)
                            if step == 6:
                                turn_out(0)
                    weigh2(1, 7)
                    if not last:
                        turn_q_with_max(J + 1)
                    turn_out(1)

                turn_q(b * HPG)
                max_pieces(b * HPG, None)
                turn_q_with_max(b * HPG)
                with pe.Fori(0, HPG - 1) as j:
                    heads_of(j, False)
                heads_of(HPG - 1, True)
                pe.wait_ge(s["ao"], 1 + b * (2 * HPG) + 2 * HPG)
                transposes(AO, 0).then_inc(s["aoT"], 1)
                pe.wait_ge(s["aoTc"], b + 1)
                for t in range(NT):
                    last = mm(SC[:, 1, t * 128:(t + 1) * 128], HT[:, t * 128:(t + 1) * 128], WOT[:, :], start=True, stop=True)
                last.then_inc(s["wo2"], 1)
                pe.wait_ge(s["h4"], b + 1)
                transposes(HA, 0).then_inc(s["h4T"], 1)
                pe.wait_ge(s["h4Tc"], b + 1)
                for t in range(NT):
                    last = mm(XP[:, t * E:(t + 1) * E], HT[:, t * 128:(t + 1) * 128], gates[:, :], start=True, stop=True)
                last.then_inc(s["lg"], 1)

                def up(e, k, t):
                    n = b * E + e
                    if t == 0:
                        pe.wait_ge(s["wcopy"], n + 1)
                    if t >= 2:
                        pe.wait_ge(s["g"], n * 4 + t - 1)
                    c, f = t // 2, t % 2
                    w = W13S[k % 2]
                    mm(SC[:, t % 2, 0:CH], w[:, f * 128:(f + 1) * 128], HT[:, c * CH:(c + 1) * CH], start=True, stop=True)
                    mm(SC[:, t % 2, CH:2 * CH], w[:, FFN + f * 128:FFN + (f + 1) * 128], HT[:, c * CH:(c + 1) * CH],
                       start=True, stop=True).then_inc(s["up"], 1)

                def down(e, k, c):
                    n = b * E + e
                    pe.wait_ge(s["g"], n * 4 + 2 * c + 2)
                    pe.wait_ge(s["accfree"], n * 2 + c + 1)
                    for t in range(4):
                        for f in range(2):
                            last = mm(MX[:, c * CH + t * 128:c * CH + (t + 1) * 128], G[:, c, f, t * 128:(t + 1) * 128],
                                      W2S[k % 2][:, f * D:(f + 1) * D], start=(f == 0), stop=(f == 1))
                    last.then_inc(s["down"] if c == 0 else s["slot"], 1)

                def expert(e, k, last):
                    up(e, k, 1)
                    up(e, k, 2)
                    down(e, k, 0)
                    up(e, k, 3)
                    if not last:
                        pe.wait_ge(s["g"], (b * E + e) * 4 + 3)
                        up(e + 1, k + 1, 0)
                    down(e, k, 1)

                up(0, 0, 0)
                with pe.Fori(0, E // 2 - 1) as ee:
                    for k in range(2):
                        expert(ee * 2 + k, k, False)
                for e in (E - 2, E - 1):
                    expert(e, e % 2, e == E - 1)


_INS = ["L0_attn_x", "L0_attn_Wq", "L0_attn_bq", "L0_attn_Wk", "L0_attn_bk", "L0_attn_Wv", "L0_attn_bv", "L0_attn_Wo",
        "L0_attn_bo", "L0_ffn_ln1_w", "L0_ffn_ln2_w", "L0_ffn_wqkv", "L0_ffn_wo", "L0_ffn_gate_w", "L0_ffn_w13",
        "L0_ffn_w2", "L0_c", "L0_wmod"]


def kernel(**inputs):
    import numpy as np
    import concourse.bacc as bacc
    from concourse.bass_utils import run_bass_kernel_spmd

    nc = bacc.Bacc("TRN2", target_bir_lowering=False, num_devices=1)
    lay = {
        "L0_attn_bq": lambda a: a.reshape(PAIRS, 128).T,
        "L0_ffn_wqkv": lambda a: a.T,
        "L0_ffn_wo": lambda a: a.T,
        "L0_ffn_gate_w": lambda a: a.T,
        "L0_ffn_w13": lambda a: a.transpose(2, 0, 1),
        "L0_ffn_w2": lambda a: a.reshape(E, D, 2, 128).transpose(3, 0, 2, 1).reshape(128, E, 2 * D),
        "L0_c": lambda a: a.T,
    }
    arrays, args = {}, []
    for name in _INS:
        a = np.asarray(inputs[name])
        a = np.ascontiguousarray(lay[name](a) if name in lay else a)
        arrays["in_" + name] = a
        args.append(nc.dram_tensor("in_" + name, a.shape, mybir.dt.from_np(a.dtype), kind="ExternalInput").ap())
    inv = (np.float32(1.0) / np.float32(10000.0) ** (np.arange(0, HD, 2, dtype=np.float32) / np.float32(HD))).astype(np.float32)
    ang = np.arange(S, dtype=np.float32)[:, None] * inv[None, :]
    cos, sin = np.cos(ang), np.sin(ang)
    rope = np.stack([np.concatenate([cos, cos], 1), np.concatenate([-sin, sin], 1)], 1).astype(np.float32)
    arrays["rope"] = rope
    args.append(nc.dram_tensor("rope", rope.shape, F32, kind="ExternalInput").ap())
    out = nc.dram_tensor("out_0", (B, S, D), F32, kind="ExternalOutput").ap()
    build(nc, *args, out)
    r = run_bass_kernel_spmd(nc, [arrays], core_ids=[0])
    return r.results[0]["out_0"]
```
